# Optimizing a Trainium2 kernel written in Bass

```python
import numpy as np
import jax
import jax.numpy as jnp

def _softmax(x, axis=-1):
    return jax.nn.softmax(x, axis=axis)

def _gelu(x):
    return jax.nn.gelu(x, approximate=True)

def _silu(x):
    return jax.nn.silu(x)

def _sigmoid(x):
    return jax.nn.sigmoid(x)

def _layernorm(x, axis=-1, eps=1e-05):
    m = jnp.mean(x, axis=axis, keepdims=True)
    v = jnp.var(x, axis=axis, keepdims=True)
    return (x - m) / jnp.sqrt(v + eps)

def _scatter_add(tgt, idx, src, axis=0):
    return tgt.at[idx].add(src)

def _segment_sum(src, seg, n):
    return jax.ops.segment_sum(src, seg, n)
kernel_name = 'mk_dlrm_tower_d1_rec_r8_eb191a'

def setup_inputs(seed: int=0):
    np.random.seed(seed)
    _w = jnp.asarray

    def _rec_inputs():
        import jax
        import jax.numpy as jnp
        _tk = jax.random.key(seed)
        dense_ctx = jax.random.normal(jax.random.fold_in(_tk, 190), (1024, 16), jnp.float32)
        ids = jnp.stack([jax.random.randint(jax.random.fold_in(_tk, 200 + f), (1024,), 0, v, jnp.int32) for f, v in enumerate([12500, 12500, 125000, 12500, 1000, 1250, 1250, 12500, 1250, 12500, 125000, 125000, 12500, 1000, 125000, 125000, 125000, 1000, 125000, 1250, 1250, 12500, 1000, 1000, 1000, 1000, 12500, 125000, 1250, 125000, 1000, 1250, 1000, 12500, 12500, 12500, 1250, 1250, 125000])], axis=1)
        tbl_0 = 0.05 * jax.random.normal(jax.random.fold_in(_tk, 500 + 0), (12500, 16), jnp.float32)
        tbl_1 = 0.05 * jax.random.normal(jax.random.fold_in(_tk, 500 + 1), (12500, 16), jnp.float32)
        tbl_2 = 0.05 * jax.random.normal(jax.random.fold_in(_tk, 500 + 2), (125000, 16), jnp.float32)
        tbl_3 = 0.05 * jax.random.normal(jax.random.fold_in(_tk, 500 + 3), (12500, 16), jnp.float32)
        tbl_4 = 0.05 * jax.random.normal(jax.random.fold_in(_tk, 500 + 4), (1000, 16), jnp.float32)
        tbl_5 = 0.05 * jax.random.normal(jax.random.fold_in(_tk, 500 + 5), (1250, 16), jnp.float32)
        tbl_6 = 0.05 * jax.random.normal(jax.random.fold_in(_tk, 500 + 6), (1250, 16), jnp.float32)
        tbl_7 = 0.05 * jax.random.normal(jax.random.fold_in(_tk, 500 + 7), (12500, 16), jnp.float32)
        tbl_8 = 0.05 * jax.random.normal(jax.random.fold_in(_tk, 500 + 8), (1250, 16), jnp.float32)
        tbl_9 = 0.05 * jax.random.normal(jax.random.fold_in(_tk, 500 + 9), (12500, 16), jnp.float32)
        tbl_10 = 0.05 * jax.random.normal(jax.random.fold_in(_tk, 500 + 10), (125000, 16), jnp.float32)
        tbl_11 = 0.05 * jax.random.normal(jax.random.fold_in(_tk, 500 + 11), (125000, 16), jnp.float32)
        tbl_12 = 0.05 * jax.random.normal(jax.random.fold_in(_tk, 500 + 12), (12500, 16), jnp.float32)
        tbl_13 = 0.05 * jax.random.normal(jax.random.fold_in(_tk, 500 + 13), (1000, 16), jnp.float32)
        tbl_14 = 0.05 * jax.random.normal(jax.random.fold_in(_tk, 500 + 14), (125000, 16), jnp.float32)
        tbl_15 = 0.05 * jax.random.normal(jax.random.fold_in(_tk, 500 + 15), (125000, 16), jnp.float32)
        tbl_16 = 0.05 * jax.random.normal(jax.random.fold_in(_tk, 500 + 16), (125000, 16), jnp.float32)
        tbl_17 = 0.05 * jax.random.normal(jax.random.fold_in(_tk, 500 + 17), (1000, 16), jnp.float32)
        tbl_18 = 0.05 * jax.random.normal(jax.random.fold_in(_tk, 500 + 18), (125000, 16), jnp.float32)
        tbl_19 = 0.05 * jax.random.normal(jax.random.fold_in(_tk, 500 + 19), (1250, 16), jnp.float32)
        tbl_20 = 0.05 * jax.random.normal(jax.random.fold_in(_tk, 500 + 20), (1250, 16), jnp.float32)
        tbl_21 = 0.05 * jax.random.normal(jax.random.fold_in(_tk, 500 + 21), (12500, 16), jnp.float32)
        tbl_22 = 0.05 * jax.random.normal(jax.random.fold_in(_tk, 500 + 22), (1000, 16), jnp.float32)
        tbl_23 = 0.05 * jax.random.normal(jax.random.fold_in(_tk, 500 + 23), (1000, 16), jnp.float32)
        tbl_24 = 0.05 * jax.random.normal(jax.random.fold_in(_tk, 500 + 24), (1000, 16), jnp.float32)
        tbl_25 = 0.05 * jax.random.normal(jax.random.fold_in(_tk, 500 + 25), (1000, 16), jnp.float32)
        tbl_26 = 0.05 * jax.random.normal(jax.random.fold_in(_tk, 500 + 26), (12500, 16), jnp.float32)
        tbl_27 = 0.05 * jax.random.normal(jax.random.fold_in(_tk, 500 + 27), (125000, 16), jnp.float32)
        tbl_28 = 0.05 * jax.random.normal(jax.random.fold_in(_tk, 500 + 28), (1250, 16), jnp.float32)
        tbl_29 = 0.05 * jax.random.normal(jax.random.fold_in(_tk, 500 + 29), (125000, 16), jnp.float32)
        tbl_30 = 0.05 * jax.random.normal(jax.random.fold_in(_tk, 500 + 30), (1000, 16), jnp.float32)
        tbl_31 = 0.05 * jax.random.normal(jax.random.fold_in(_tk, 500 + 31), (1250, 16), jnp.float32)
        tbl_32 = 0.05 * jax.random.normal(jax.random.fold_in(_tk, 500 + 32), (1000, 16), jnp.float32)
        tbl_33 = 0.05 * jax.random.normal(jax.random.fold_in(_tk, 500 + 33), (12500, 16), jnp.float32)
        tbl_34 = 0.05 * jax.random.normal(jax.random.fold_in(_tk, 500 + 34), (12500, 16), jnp.float32)
        tbl_35 = 0.05 * jax.random.normal(jax.random.fold_in(_tk, 500 + 35), (12500, 16), jnp.float32)
        tbl_36 = 0.05 * jax.random.normal(jax.random.fold_in(_tk, 500 + 36), (1250, 16), jnp.float32)
        tbl_37 = 0.05 * jax.random.normal(jax.random.fold_in(_tk, 500 + 37), (1250, 16), jnp.float32)
        tbl_38 = 0.05 * jax.random.normal(jax.random.fold_in(_tk, 500 + 38), (125000, 16), jnp.float32)
        _rk = jax.random.fold_in(_tk, 7)
        W_top1 = 0.05 * jax.random.normal(jax.random.fold_in(_tk, 801), (400, 512), jnp.float32)
        W_top2 = 0.0441942 * jax.random.normal(jax.random.fold_in(_tk, 802), (512, 256), jnp.float32)
        W_top3 = 0.0625 * jax.random.normal(jax.random.fold_in(_tk, 803), (256, 1), jnp.float32)
        b_top1 = jnp.zeros((512,), jnp.float32)
        b_top2 = jnp.zeros((256,), jnp.float32)
        return (dense_ctx, ids, tbl_0, tbl_1, tbl_2, tbl_3, tbl_4, tbl_5, tbl_6, tbl_7, tbl_8, tbl_9, tbl_10, tbl_11, tbl_12, tbl_13, tbl_14, tbl_15, tbl_16, tbl_17, tbl_18, tbl_19, tbl_20, tbl_21, tbl_22, tbl_23, tbl_24, tbl_25, tbl_26, tbl_27, tbl_28, tbl_29, tbl_30, tbl_31, tbl_32, tbl_33, tbl_34, tbl_35, tbl_36, tbl_37, tbl_38, W_top1, b_top1, W_top2, b_top2, W_top3)
    dense_ctx, ids, tbl_0, tbl_1, tbl_2, tbl_3, tbl_4, tbl_5, tbl_6, tbl_7, tbl_8, tbl_9, tbl_10, tbl_11, tbl_12, tbl_13, tbl_14, tbl_15, tbl_16, tbl_17, tbl_18, tbl_19, tbl_20, tbl_21, tbl_22, tbl_23, tbl_24, tbl_25, tbl_26, tbl_27, tbl_28, tbl_29, tbl_30, tbl_31, tbl_32, tbl_33, tbl_34, tbl_35, tbl_36, tbl_37, tbl_38, W_top1, b_top1, W_top2, b_top2, W_top3 = _rec_inputs()

    def _L0_rec_setup():
        import jax, jax.numpy as jnp
        import numpy as np
        B, F0, D = (256, 39, 16)
        CROSS = [128, 128, 128]
        key = jax.random.key(seed)
        k0, k1, k2, k3 = jax.random.split(key, 4)
        inputs = jax.random.normal(k0, (B, F0, D), dtype=jnp.float32)
        f0 = jax.random.normal(k1, (F0 * F0, CROSS[0]), dtype=jnp.float32) * 0.05
        f1 = jax.random.normal(k2, (CROSS[0] * F0, CROSS[1]), dtype=jnp.float32) * 0.05
        f2 = jax.random.normal(k3, (CROSS[1] * F0, CROSS[2]), dtype=jnp.float32) * 0.05
        return {'inputs': inputs, 'f0': f0, 'f1': f1, 'f2': f2}
    _L0_rec_all = _L0_rec_setup()
    _L0_rec_in = {k: v for k, v in _L0_rec_all.items() if k in ('f0', 'f1', 'f2')}
    del _L0_rec_all
    return {'dense_ctx': dense_ctx, 'ids': ids, 'tbl_0': tbl_0, 'tbl_1': tbl_1, 'tbl_2': tbl_2, 'tbl_3': tbl_3, 'tbl_4': tbl_4, 'tbl_5': tbl_5, 'tbl_6': tbl_6, 'tbl_7': tbl_7, 'tbl_8': tbl_8, 'tbl_9': tbl_9, 'tbl_10': tbl_10, 'tbl_11': tbl_11, 'tbl_12': tbl_12, 'tbl_13': tbl_13, 'tbl_14': tbl_14, 'tbl_15': tbl_15, 'tbl_16': tbl_16, 'tbl_17': tbl_17, 'tbl_18': tbl_18, 'tbl_19': tbl_19, 'tbl_20': tbl_20, 'tbl_21': tbl_21, 'tbl_22': tbl_22, 'tbl_23': tbl_23, 'tbl_24': tbl_24, 'tbl_25': tbl_25, 'tbl_26': tbl_26, 'tbl_27': tbl_27, 'tbl_28': tbl_28, 'tbl_29': tbl_29, 'tbl_30': tbl_30, 'tbl_31': tbl_31, 'tbl_32': tbl_32, 'tbl_33': tbl_33, 'tbl_34': tbl_34, 'tbl_35': tbl_35, 'tbl_36': tbl_36, 'tbl_37': tbl_37, 'tbl_38': tbl_38, 'W_top1': W_top1, 'b_top1': b_top1, 'W_top2': W_top2, 'b_top2': b_top2, 'W_top3': W_top3, 'L0_rec_f0': _L0_rec_in['f0'], 'L0_rec_f1': _L0_rec_in['f1'], 'L0_rec_f2': _L0_rec_in['f2']}

def reference(dense_ctx, ids, tbl_0, tbl_1, tbl_2, tbl_3, tbl_4, tbl_5, tbl_6, tbl_7, tbl_8, tbl_9, tbl_10, tbl_11, tbl_12, tbl_13, tbl_14, tbl_15, tbl_16, tbl_17, tbl_18, tbl_19, tbl_20, tbl_21, tbl_22, tbl_23, tbl_24, tbl_25, tbl_26, tbl_27, tbl_28, tbl_29, tbl_30, tbl_31, tbl_32, tbl_33, tbl_34, tbl_35, tbl_36, tbl_37, tbl_38, W_top1, b_top1, W_top2, b_top2, W_top3, L0_rec_f0, L0_rec_f1, L0_rec_f2):
    import jax
    import jax.numpy as jnp

    def _L0_rec_ref(inputs, f0, f1, f2):
        import jax, jax.numpy as jnp
        import numpy as np
        B, F0, D = (256, 39, 16)
        CROSS = [128, 128, 128]
        filters = [f0, f1, f2]
        x0 = inputs
        xk = inputs
        outs = []
        for W in filters:
            b, f, d = x0.shape
            g = xk.shape[1]
            z = jnp.einsum('bfd,bgd->bfgd', x0, xk).reshape(b, f * g, d)
            cur = jnp.einsum('bpd,pm->bmd', z, W)
            outs.append(cur)
            xk = cur
        result = jnp.concatenate(outs, axis=1)
        return jnp.sum(result, axis=-1)
    e = jnp.stack([tbl_0[ids[:, 0]], tbl_1[ids[:, 1]], tbl_2[ids[:, 2]], tbl_3[ids[:, 3]], tbl_4[ids[:, 4]], tbl_5[ids[:, 5]], tbl_6[ids[:, 6]], tbl_7[ids[:, 7]], tbl_8[ids[:, 8]], tbl_9[ids[:, 9]], tbl_10[ids[:, 10]], tbl_11[ids[:, 11]], tbl_12[ids[:, 12]], tbl_13[ids[:, 13]], tbl_14[ids[:, 14]], tbl_15[ids[:, 15]], tbl_16[ids[:, 16]], tbl_17[ids[:, 17]], tbl_18[ids[:, 18]], tbl_19[ids[:, 19]], tbl_20[ids[:, 20]], tbl_21[ids[:, 21]], tbl_22[ids[:, 22]], tbl_23[ids[:, 23]], tbl_24[ids[:, 24]], tbl_25[ids[:, 25]], tbl_26[ids[:, 26]], tbl_27[ids[:, 27]], tbl_28[ids[:, 28]], tbl_29[ids[:, 29]], tbl_30[ids[:, 30]], tbl_31[ids[:, 31]], tbl_32[ids[:, 32]], tbl_33[ids[:, 33]], tbl_34[ids[:, 34]], tbl_35[ids[:, 35]], tbl_36[ids[:, 36]], tbl_37[ids[:, 37]], tbl_38[ids[:, 38]]], axis=1)
    z = _L0_rec_ref(e, L0_rec_f0, L0_rec_f1, L0_rec_f2)
    z = z.reshape(z.shape[0], -1)
    h = jnp.concatenate([z, dense_ctx], axis=1)
    h = jnp.maximum(h @ W_top1 + b_top1, 0.0)
    h = jnp.maximum(h @ W_top2 + b_top2, 0.0)
    y = h @ W_top3
    return y

_drawn_inputs = setup_inputs


def setup_inputs(seed=0):
    import zlib

    import numpy as np

    out = dict(_drawn_inputs(seed))
    spreads = {'b_top1': (0.0, 0.566), 'b_top2': (0.0, 0.1)}
    factors = {'tbl_0': 4.454,
     'tbl_1': 4.719,
     'tbl_2': 4.728,
     'tbl_3': 5.007,
     'tbl_4': 4.876,
     'tbl_5': 4.884,
     'tbl_6': 4.847,
     'tbl_7': 4.815,
     'tbl_8': 4.935,
     'tbl_9': 4.569,
     'tbl_10': 5.1,
     'tbl_11': 4.552,
     'tbl_12': 4.261,
     'tbl_13': 4.464,
     'tbl_14': 4.4,
     'tbl_15': 4.824,
     'tbl_16': 5.047,
     'tbl_17': 4.797,
     'tbl_18': 5.097,
     'tbl_19': 4.865,
     'tbl_20': 4.922,
     'tbl_21': 4.914,
     'tbl_22': 4.447,
     'tbl_23': 4.604,
     'tbl_24': 4.557,
     'tbl_25': 4.516,
     'tbl_26': 4.786,
     'tbl_27': 5.022,
     'tbl_28': 4.66,
     'tbl_29': 4.95,
     'tbl_30': 4.858,
     'tbl_31': 4.302,
     'tbl_32': 4.796,
     'tbl_33': 4.766,
     'tbl_34': 4.292,
     'tbl_35': 4.626,
     'tbl_36': 4.879,
     'tbl_37': 4.841,
     'tbl_38': 4.907,
     'L0_rec_f1': 5.15,
     'L0_rec_f2': 8.0}
    for name, (base, spread) in spreads.items():
        noise = np.random.default_rng([zlib.crc32(name.encode()), seed]).standard_normal(out[name].shape)
        drawn = base * np.exp(spread * noise) if base else spread * noise
        out[name] = jnp.asarray(drawn.astype(out[name].dtype))
    for name, factor in factors.items():
        out[name] = (out[name] * factor).astype(out[name].dtype)
    return out
```

```python
import concourse.bass as bass
from concourse import mybir
from contextlib import ExitStack

FP32 = mybir.dt.float32
F32R = mybir.dt.float32r
I32 = mybir.dt.int32
ALU = mybir.AluOpType
ACT = mybir.ActivationFunctionType
AX = mybir.AxisListType

B, F, D, H = 1024, 39, 16, 128
N1, N2, ND = 512, 256, 16
P = 128
BLK_B = P // D
TILE_B = 4 * BLK_B
QUADS = B // P
TILES, BLOCKS = 4, 16
COLS = 4 * P

REP = 3
ONE = REP * F
HI = ONE + 1
LO = HI + F
ROW = LO + F
FX = F + 1

SHIFTS = [*range(1, F // 2 + 1), 0]
PAIRK = (len(SHIFTS) + REP - 1) // REP
LAST_ROWS = (len(SHIFTS) - REP * (PAIRK - 1)) * F

PIECES = 10
A_PIECES = [1, 3, 6, 8]
D_PIECES = [q for q in range(PIECES) if q not in A_PIECES]
D_OPS = sum(min(4, F - 4 * q) for q in D_PIECES)
A_F = 4 * len(A_PIECES)
ACC = 4
PARTS = A_F + ACC
TREE = 5
D_BANKS, A_BANKS = 3, 2

S_TA, S_TS = 1, 3
S_SEL = [6 + 4 * k for k in range(PAIRK)]
S_PAIR = [9 + 4 * k for k in range(PAIRK)]
S_L3, S_H1, S_H2, S_Y = 20, 24, 27, 30


def g_slots(tile):
    return {8: -2, 18: -1, (33 if tile == 0 else 28): 0, 38: 1}


GATHER_PER_BLOCK = 4


def cin_kernel(nc, t, tables, out):
    ctx = ExitStack()
    with ctx:
        def sb(name, shape, dt=FP32):
            return ctx.enter_context(nc.sbuf_tensor(name, shape, dt))

        def bank(name):
            return ctx.enter_context(nc.psum_tensor(name, [P, 512], FP32))

        def sem(name):
            return ctx.enter_context(nc.semaphore(name))

        ident = sb("ident", [P, P])
        blockmask = sb("blockmask", [P, BLK_B])
        sel_raw = sb("sel_raw", [2 * F, PAIRK * REP * F])
        sel = sb("sel", [2 * F, PAIRK, REP * F], F32R)
        w0 = sb("w0", [REP * F, PAIRK, H])
        w0_swapped = sb("w0_swapped", [REP * F, PAIRK, H])
        w1 = sb("w1", [P, F, H])
        w1_hi = sb("w1_hi", [P, F * H], F32R)
        w1_lo = sb("w1_lo", [P, F * H], F32R)
        w2 = sb("w2", [P, F, H])
        wt1 = sb("wt1", [P, 3, N1])
        wt1_dense = sb("wt1_dense", [ND, N1])
        wt2 = sb("wt2", [P, N1 // P, N2])
        wt3 = sb("wt3", [P, N2 // P])
        bt1 = sb("bt1", [P, N1 // P])
        bt2 = sb("bt2", [P, N2 // P])
        dense = sb("dense", [ND, B])
        ids = sb("ids", [P, QUADS, F], I32)
        emb = sb("emb", [P, F, D])
        emb_rows = sb("emb_rows", [P, D, ROW])
        x_cols = [sb(f"x_cols{i}", [P, 4, ROW]) for i in range(TILES)]
        x_rep = sb("x_rep", [REP * F, COLS])
        x_parts = sb("x_parts", [2 * F, COLS], F32R)
        pairs = [sb(f"pairs{i}", [REP * F, COLS]) for i in range(2)]
        cur1_hi = [sb(f"cur1_hi{i}", [P, COLS], F32R) for i in range(2)]
        cur1_lo = [sb(f"cur1_lo{i}", [P, COLS], F32R) for i in range(2)]
        parts = [sb(f"parts{i}", [P, PARTS, H]) for i in range(2)]
        cur2 = [sb(f"cur2_{i}", [P, H]) for i in range(2)]
        x_diag = [sb(f"x_diag{i}", [P, FX, BLK_B]) for i in range(2)]
        G = sb("G", [P, TILES, FX, TILE_B])
        sum1 = sb("sum1", [P, B])
        sum3 = sb("sum3", [P, P])
        h1 = sb("h1", [P, N1 // P, P])
        h2 = sb("h2", [P, N2 // P, P])
        y = sb("y", [1, B])
        l2d = [bank(f"l2d{i}") for i in range(D_BANKS)]
        l2a = [bank(f"l2a{i}") for i in range(A_BANKS)]
        xbank = bank("xbank")
        cur1_bank = bank("cur1_bank")
        gbank = bank("gbank")

        x_rows = t["x_rows"]

        const_loaded = sem("const_loaded")
        w0_loaded = sem("w0_loaded")
        w1_loaded = sem("w1_loaded")
        top_loaded = sem("top_loaded")
        ids_loaded = sem("ids_loaded")
        sel_ready = sem("sel_ready")
        w0_ready = sem("w0_ready")
        w1_hi_ready = sem("w1_hi_ready")
        w1_lo_ready = sem("w1_lo_ready")
        gathered = sem("gathered")
        rows_copied = sem("rows_copied")
        rows_low = sem("rows_low")
        rows_stored = sem("rows_stored")
        ones_set = sem("ones_set")
        x_loaded = [sem(f"x_loaded{i}") for i in range(TILES)]
        transposed = sem("transposed")
        x_rep_ready = sem("x_rep_ready")
        x_parts_ready = sem("x_parts_ready")
        selected = sem("selected")
        pairs_ready = sem("pairs_ready")
        pairs_used = sem("pairs_used")
        cur1_hi_ready = sem("cur1_hi_ready")
        cur1_lo_ready = sem("cur1_lo_ready")
        sum1_ready = sem("sum1_ready")
        l2d_ready = sem("l2d_ready")
        l2a_ready = sem("l2a_ready")
        acc_done = sem("acc_done")
        prod_done = sem("prod_done")
        tree_done = sem("tree_done")
        x_diag_ready = sem("x_diag_ready")
        g_ready = sem("g_ready")
        g_copied = sem("g_copied")
        l3_ready = sem("l3_ready")
        l3_copied = sem("l3_copied")
        h1_ready = sem("h1_ready")
        h1_copied = sem("h1_copied")
        h2_ready = sem("h2_ready")
        h2_copied = sem("h2_copied")
        y_ready = sem("y_ready")
        y_copied = sem("y_copied")
        out_stored = sem("out_stored")

        block = ctx.enter_context(nc.Block())

        def wait(eng, s, value):
            if not isinstance(value, int) or value > 0:
                eng.wait_ge(s, value)

        def value(eng, v):
            if not isinstance(v, int):
                eng.compute_val(v)
            return v

        def over_quads(eng, quad):
            quad(0, True, False)
            with eng.Fori(1, QUADS - 1) as u:
                quad(u, False, False)
            quad(QUADS - 1, False, True)

        @block.sync
        def _(sp):
            sp.dma_start(ids[:], t["ids"].rearrange("(u p) f -> p u f", p=P)).then_inc(ids_loaded, 16)
            sp.dma_start(w1[:], t["w1"].rearrange("(f g) m -> g f m", g=H)).then_inc(w1_loaded, 16)
            sp.dma_start(ident[:], t["ident"]).then_inc(const_loaded, 16)
            sp.dma_start(blockmask[:], t["blockmask"]).then_inc(const_loaded, 16)
            sp.dma_start(sel_raw[:], t["sel"]).then_inc(const_loaded, 16)
            whole = REP * F * (PAIRK - 1)
            for dst, src, rows in ((w0, t["w0"], LAST_ROWS), (w0_swapped, t["w0_swapped"], LAST_ROWS - F)):
                sp.dma_start(dst[:, 0:PAIRK - 1, :],
                             src[0:whole, :].rearrange("(k p) m -> p k m", p=REP * F)).then_inc(w0_loaded, 16)
                sp.dma_start(dst[0:rows, PAIRK - 1, :], src[whole:whole + rows, :]).then_inc(w0_loaded, 16)

            def store_rows(u):
                row, copied = value(sp, u * (P * D)), value(sp, u + 1)
                sp.wait_ge(rows_copied, copied)
                sp.wait_ge(rows_low, copied)
                sp.dma_start(x_rows[bass.ds(row, P * D), :].rearrange("(b d) r -> b (d r)", d=D),
                             emb_rows[:].rearrange("p d r -> p (d r)")).then_inc(rows_stored, 16)

            def load_tile(u, i):
                row = value(sp, u * (P * D) + i * COLS)
                diag_used = value(sp, (u - 1) * BLOCKS + 4 * (i + 1))
                weighed = value(sp, ((u - 1) * BLOCKS + 4 * (i + 1)) * len(A_PIECES))
                stored = value(sp, (u + 1) * 16)
                wait(sp, x_diag_ready, diag_used)
                wait(sp, prod_done, weighed)
                wait(sp, rows_stored, stored)
                sp.dma_start(x_cols[i][:], x_rows[bass.ds(row, COLS), :].rearrange("(j c) r -> c j r", c=P)
                             ).then_inc(x_loaded[i], 16)

            store_rows(0)
            load_tile(0, 0)
            load_tile(0, 1)
            sp.dma_start(w2[:], t["w2"].rearrange("(f g) m -> g f m", g=H)).then_inc(top_loaded, 16)
            sp.dma_start(wt1[:], t["wt1"][0:3 * P, :].rearrange("(k p) n -> p k n", p=P)).then_inc(top_loaded, 16)
            sp.dma_start(wt1_dense[:], t["wt1"][3 * P:3 * P + ND, :]).then_inc(top_loaded, 16)
            sp.dma_start(wt2[:], t["wt2"].rearrange("(k p) n -> p k n", p=P)).then_inc(top_loaded, 16)
            sp.dma_start(wt3[:], t["wt3"]).then_inc(top_loaded, 16)
            sp.dma_start(bt1[:], t["bt1"]).then_inc(top_loaded, 16)
            sp.dma_start(bt2[:], t["bt2"]).then_inc(top_loaded, 16)
            sp.dma_start(dense[:], t["dense"]).then_inc(top_loaded, 16)

            def quad(u, first, last):
                load_tile(u, 2)
                load_tile(u, 3)
                if not last:
                    store_rows(u + 1)
                    load_tile(u + 1, 0)
                    load_tile(u + 1, 1)

            over_quads(sp, quad)
            sp.wait_ge(y_copied, QUADS)
            sp.dma_start(out, y[:]).then_inc(out_stored, 16)
            sp.wait_ge(out_stored, 16)

        @block.gpsimd
        def _(pool):
            def gather(u, f):
                pool.indirect_dma_start(
                    emb[:, f, :], None, tables[f],
                    bass.IndirectOffsetOnAxis(ap=next_ids[:, f:f + 1], axis=0)).then_inc(gathered, 16)

            def add_parts(u, n):
                g, v, c = u * BLOCKS + n, parts[n % 2], cur2[n % 2]
                pool.wait_ge(prod_done, (g + 1) * len(A_PIECES))
                pool.wait_ge(acc_done, (g + 1) * D_OPS)
                wait(pool, g_ready, g - 1)
                steps = [(v[:, 0:10], v[:, 0:10], v[:, 10:20]), (v[:, 0:5], v[:, 0:5], v[:, 5:10]),
                         (v[:, 0:2], v[:, 0:2], v[:, 2:4]), (v[:, 0], v[:, 0], v[:, 1]), (c[:], v[:, 0], v[:, 4])]
                for i, (o, a, b) in enumerate(steps):
                    if i:
                        pool.wait_ge(tree_done, g * TREE + i)
                    pool.tensor_tensor(o, a, b, ALU.add).then_inc(tree_done, 1)

            next_ids = sb("next_ids", [P, F], I32)
            ids_moved = sem("ids_moved")

            def move_ids(u):
                pool.tensor_copy(next_ids[:], ids[:, u, :]).then_inc(ids_moved, 1)
                pool.wait_ge(ids_moved, u + 1)

            pool.memset(emb_rows[:, :, ONE:ONE + 1], 1.0).then_inc(ones_set, 1)
            pool.wait_ge(ids_loaded, 16)
            move_ids(0)
            for f in range(F):
                gather(0, f)

            def quad(u, first, last):
                for n in range(BLOCKS):
                    if not last:
                        if n == 0:
                            pool.wait_ge(gathered, (u + 1) * F * 16)
                            pool.wait_ge(rows_copied, u + 1)
                            pool.wait_ge(rows_low, u + 1)
                            move_ids(u + 1)
                    add_parts(u, n)
                    if not last:
                        for f in range(GATHER_PER_BLOCK * n, min(F, GATHER_PER_BLOCK * (n + 1))):
                            gather(u + 1, f)

            over_quads(pool, quad)

        @block.scalar
        def _(act):
            def copy_rows(u):
                act.wait_ge(gathered, (u + 1) * F * 16)
                wait(act, rows_stored, u * 16)
                src = emb[:].rearrange("p f d -> p d f")
                for r in range(REP):
                    nc.scalar.activation(emb_rows[:, :, r * F:(r + 1) * F], src, ACT.Copy)
                nc.scalar.activation(emb_rows[:, :, HI:LO].bitcast(F32R), src, ACT.Copy).then_inc(rows_copied, 1)

            def weigh_piece(u, n, q):
                g, i = u * BLOCKS + n, A_PIECES.index(q)
                k = g * len(A_PIECES) + i
                if i == 0:
                    wait(act, tree_done, (g - 1) * TREE)
                    act.wait_ge(x_loaded[n // 4], (u + 1) * 16)
                act.wait_ge(l2a_ready, k + 1)
                src = l2a[(n * len(A_PIECES) + i) % A_BANKS]
                for r in range(4):
                    f = 4 * q + r
                    last = nc.scalar.activation(parts[n % 2][:, 4 * i + r, :], src[:, r * H:(r + 1) * H], ACT.Copy,
                                                scale=x_cols[n // 4][:, n % 4, f:f + 1])
                last.then_inc(prod_done, 1)

            def copy_x_rep(tile):
                act.wait_ge(transposed, 2 * tile + 1)
                wait(act, pairs_ready, tile * PAIRK)
                nc.scalar.activation(x_rep[:], xbank[0:REP * F, :], ACT.Copy).then_inc(x_rep_ready, 1)

            def copy_x_parts(tile):
                act.wait_ge(transposed, 2 * tile + 2)
                wait(act, selected, tile * PAIRK)
                nc.scalar.activation(x_parts[:], xbank[0:2 * F, :], ACT.Copy).then_inc(x_parts_ready, 1)

            def copy_cur1_hi(tile, i):
                act.wait_ge(pairs_used, (tile + 1) * PAIRK)
                wait(act, l2d_ready, (tile - 1) * 4 * len(D_PIECES))
                nc.scalar.activation(cur1_hi[i % 2][:], cur1_bank[:], ACT.Copy).then_inc(cur1_hi_ready, 1)

            def copy_g(u, n):
                g = u * BLOCKS + n
                act.wait_ge(g_ready, g + 1)
                if n == 0:
                    wait(act, h1_ready, u)
                dst = G[:, n // 4, :, (n % 4) * BLK_B:(n % 4 + 1) * BLK_B]
                nc.scalar.activation(dst, gbank[:, 0:FX * BLK_B].rearrange("p (f b) -> p f b", b=BLK_B),
                                     ACT.Copy).then_inc(g_copied, 1)

            def copy_l3(u):
                act.wait_ge(l3_ready, u + 1)
                wait(act, h1_ready, u)
                nc.scalar.activation(sum3[:], gbank[:, 0:P], ACT.Copy).then_inc(l3_copied, 1)

            def relu(u, ready, used, dst, bias, done):
                act.wait_ge(ready, u + 1)
                wait(act, used, u)
                for m in range(dst.shape[1]):
                    last = nc.scalar.activation(dst[:, m, :], gbank[:, m * P:(m + 1) * P], ACT.Relu,
                                                bias=bias[:, m:m + 1])
                last.then_inc(done, 1)

            def relu1(u):
                relu(u, h1_ready, h2_ready, h1, bt1, h1_copied)

            def relu2(u):
                relu(u, h2_ready, y_ready, h2, bt2, h2_copied)

            def copy_y(u):
                act.wait_ge(y_ready, u + 1)
                nc.scalar.activation(y[:, bass.ds(u * P, P)], gbank[0:1, 0:P], ACT.Copy).then_inc(y_copied, 1)

            act.wait_ge(w1_loaded, 16)
            nc.scalar.activation(w1_hi[:], w1[:].rearrange("p f m -> p (f m)"), ACT.Copy).then_inc(w1_hi_ready, 1)
            act.wait_ge(ones_set, 1)
            copy_rows(0)
            copy_x_rep(0)
            copy_x_parts(0)
            copy_cur1_hi(0, 0)
            act.wait_ge(top_loaded, 8 * 16)

            def quad(u, first, last):
                for i in range(TILES):
                    tile, more = u * TILES + i, not (last and i == TILES - 1)
                    gs = g_slots(i)
                    for s in range(4 * PIECES):
                        n, q = 4 * i + s // PIECES, s % PIECES
                        if q in A_PIECES:
                            weigh_piece(u, n, q)
                        if more and s == S_TA:
                            copy_x_rep(tile + 1)
                        if more and s == S_TS:
                            copy_x_parts(tile + 1)
                        if s in gs:
                            b = 4 * i + gs[s]
                            if b >= 0:
                                copy_g(u, b)
                            elif not first:
                                copy_g(u - 1, BLOCKS + b)
                        if i == 0 and not first:
                            if s == S_L3 + 1:
                                copy_l3(u - 1)
                            if s == S_H1 + 1:
                                relu1(u - 1)
                            if s == S_H2 + 1:
                                relu2(u - 1)
                            if s == S_Y + 1:
                                copy_y(u - 1)
                        if i == 2 and s == 34 and not last:
                            copy_rows(u + 1)
                        if more and s == S_PAIR[-1] + 1:
                            copy_cur1_hi(tile + 1, i + 1)

            over_quads(act, quad)
            u = QUADS - 1
            copy_g(u, BLOCKS - 2)
            copy_g(u, BLOCKS - 1)
            copy_l3(u)
            relu1(u)
            relu2(u)
            copy_y(u)

        @block.vector
        def _(dve):
            def low_rows(u):
                dve.wait_ge(rows_copied, u + 1)
                nc.vector.tensor_tensor(emb_rows[:, :, LO:ROW], emb[:].rearrange("p f d -> p d f"),
                                        emb_rows[:, :, HI:LO], ALU.subtract).then_inc(rows_low, 1)

            def sum_piece(u, n, q):
                g, i = u * BLOCKS + n, D_PIECES.index(q)
                if i == 0:
                    wait(dve, tree_done, (g - 1) * TREE)
                    dve.wait_ge(x_loaded[n // 4], (u + 1) * 16)
                dve.wait_ge(l2d_ready, g * len(D_PIECES) + i + 1)
                src = l2d[(n * len(D_PIECES) + i) % D_BANKS]
                for r in range(min(4, F - 4 * q)):
                    f, e = 4 * q + r, 4 * i + r
                    acc = parts[n % 2][:, A_F + r, :]
                    x = x_cols[n // 4][:, n % 4, f:f + 1]
                    if i == 0:
                        nc.vector.tensor_scalar(acc, src[:, r * H:(r + 1) * H], x, None, ALU.mult
                                                ).then_inc(acc_done, 1)
                    else:
                        if r % 2 == 0:
                            dve.wait_ge(acc_done, g * D_OPS + min(e + 2 - ACC, D_OPS))
                        nc.vector.scalar_tensor_tensor(acc, src[:, r * H:(r + 1) * H], x, acc, ALU.mult, ALU.add
                                                       ).then_inc(acc_done, 1)

            def make_pairs(tile, k):
                rows = REP * F if k < PAIRK - 1 else LAST_ROWS
                g = tile * PAIRK + k
                if k == 0:
                    dve.wait_ge(x_rep_ready, tile + 1)
                dve.wait_ge(selected, g + 1)
                wait(dve, pairs_used, g - 1)
                nc.vector.tensor_tensor(pairs[k % 2][0:rows, :], xbank[0:rows, :], x_rep[0:rows, :], ALU.mult
                                        ).then_inc(pairs_ready, 1)

            def take_cur1(tile, col, i):
                dve.wait_ge(cur1_hi_ready, tile + 1)
                nc.vector.tensor_tensor(cur1_lo[i % 2][:], cur1_bank[:], cur1_hi[i % 2][:].bitcast(FP32),
                                        ALU.subtract).then_inc(cur1_lo_ready, 1)
                nc.vector.tensor_reduce(sum1[:, bass.ds(col, TILE_B)],
                                        cur1_bank[:].rearrange("p (b d) -> p b d", d=D), AX.X, ALU.add
                                        ).then_inc(sum1_ready, 1)

            def make_x_diag(u, n):
                g = u * BLOCKS + n
                wait(dve, g_ready, g - 1)
                x = x_cols[n // 4][:, n % 4, ONE - F:ONE + 1]
                nc.vector.tensor_tensor(x_diag[n % 2][:], x.unsqueeze(2).to_broadcast([P, FX, BLK_B]),
                                        blockmask[:].unsqueeze(1).to_broadcast([P, FX, BLK_B]), ALU.mult
                                        ).then_inc(x_diag_ready, 1)

            dve.wait_ge(const_loaded, 3 * 16)
            nc.vector.tensor_copy(sel[:].rearrange("p k m -> p (k m)"), sel_raw[:]).then_inc(sel_ready, 1)
            dve.wait_ge(w0_loaded, 4 * 16)
            nc.vector.tensor_tensor(w0[:, 0:PAIRK - 1, :], w0[:, 0:PAIRK - 1, :], w0_swapped[:, 0:PAIRK - 1, :],
                                    ALU.add)
            rows = LAST_ROWS - F
            nc.vector.tensor_tensor(w0[0:rows, PAIRK - 1, :], w0[0:rows, PAIRK - 1, :],
                                    w0_swapped[0:rows, PAIRK - 1, :], ALU.add).then_inc(w0_ready, 1)
            dve.wait_ge(w1_hi_ready, 1)
            nc.vector.tensor_tensor(w1_lo[:], w1[:].rearrange("p f m -> p (f m)"), w1_hi[:].bitcast(FP32),
                                    ALU.subtract).then_inc(w1_lo_ready, 1)
            low_rows(0)
            for k in range(PAIRK):
                make_pairs(0, k)
            take_cur1(0, 0, 0)

            def quad(u, first, last):
                for i in range(TILES):
                    tile, more = u * TILES + i, not (last and i == TILES - 1)
                    for s in range(4 * PIECES):
                        n, q = 4 * i + s // PIECES, s % PIECES
                        if q in D_PIECES:
                            sum_piece(u, n, q)
                        if q == 5:
                            if n >= 1:
                                make_x_diag(u, n - 1)
                            elif not first:
                                make_x_diag(u - 1, BLOCKS - 1)
                        if more and s - 1 in S_SEL:
                            make_pairs(tile + 1, S_SEL.index(s - 1))
                        if more and s == S_PAIR[-1] + 2:
                            take_cur1(tile + 1, (tile + 1) * TILE_B, i + 1)
                        if i == 2 and s == 38 and not last:
                            low_rows(u + 1)

            over_quads(dve, quad)
            make_x_diag(QUADS - 1, BLOCKS - 1)

        @block.tensor
        def _(pe):
            def transpose_rep(tile, u, i):
                pe.wait_ge(x_loaded[i], (u + 1) * 16)
                wait(pe, pairs_ready, tile * PAIRK)
                for j in range(4):
                    last = nc.tensor.transpose(xbank[0:REP * F, j * P:(j + 1) * P], x_cols[i][:, j, 0:REP * F],
                                               ident[:])
                last.then_inc(transposed, 1)

            def transpose_parts(tile, i):
                pe.wait_ge(x_rep_ready, tile + 1)
                for j in range(4):
                    last = nc.tensor.transpose(xbank[0:2 * F, j * P:(j + 1) * P], x_cols[i][:, j, HI:ROW], ident[:])
                last.then_inc(transposed, 1)

            def select(tile, k):
                g = tile * PAIRK + k
                if k == 0:
                    pe.wait_ge(x_parts_ready, tile + 1)
                else:
                    pe.wait_ge(pairs_ready, g)
                rows = REP * F if k < PAIRK - 1 else LAST_ROWS
                nc.tensor.matmul(xbank[0:rows, :], sel[:, k, 0:rows], x_parts[:], start=True, stop=True
                                 ).then_inc(selected, 1)

            def sum_pairs(tile, k):
                g = tile * PAIRK + k
                pe.wait_ge(pairs_ready, g + 1)
                if k == 0:
                    wait(pe, cur1_lo_ready, tile)
                    wait(pe, sum1_ready, tile)
                rows = REP * F if k < PAIRK - 1 else LAST_ROWS
                nc.tensor.matmul(cur1_bank[:], w0[0:rows, k, :], pairs[k % 2][0:rows, :], start=k == 0,
                                 stop=k == PAIRK - 1).then_inc(pairs_used, 1)

            def layer2_piece(u, n, q):
                g, on_d = u * BLOCKS + n, q in D_PIECES
                width = min(4, F - 4 * q) * H
                if on_d:
                    i = D_PIECES.index(q)
                    k = n * len(D_PIECES) + i
                    dst = l2d[k % D_BANKS]
                    back = i - D_BANKS
                    wait(pe, acc_done, g * D_OPS + 4 * (back + 1) if back >= 0 else
                         (g - 1) * D_OPS + min(4 * (back + len(D_PIECES) + 1), D_OPS))
                else:
                    i = A_PIECES.index(q)
                    k = n * len(A_PIECES) + i
                    dst = l2a[k % A_BANKS]
                    wait(pe, prod_done, g * len(A_PIECES) + i + 1 - A_BANKS)
                lo, hi = cur1_lo[n // 4 % 2], cur1_hi[n // 4 % 2]
                cols = slice(n % 4 * P, (n % 4 + 1) * P)
                ws = slice(4 * q * H, 4 * q * H + width)
                nc.tensor.matmul(dst[:, 0:width], hi[:, cols], w1_hi[:, ws], start=True, stop=False)
                nc.tensor.matmul(dst[:, 0:width], hi[:, cols], w1_lo[:, ws], start=False, stop=False)
                nc.tensor.matmul(dst[:, 0:width], lo[:, cols], w1_hi[:, ws], start=False, stop=True
                                 ).then_inc(l2d_ready if on_d else l2a_ready, 1)

            def make_g(u, n):
                g = u * BLOCKS + n
                pe.wait_ge(tree_done, (g + 1) * TREE)
                pe.wait_ge(x_diag_ready, g + 1)
                wait(pe, g_copied, g)
                if n == 0:
                    wait(pe, y_copied, u)
                nc.tensor.matmul(gbank[:, 0:FX * BLK_B], cur2[n % 2][:], x_diag[n % 2][:].rearrange("p f b -> p (f b)"),
                                 start=True, stop=True).then_inc(g_ready, 1)

            def layer3(u):
                pe.wait_ge(g_copied, (u + 1) * BLOCKS)
                for f in range(F):
                    last = nc.tensor.matmul(gbank[:, 0:P], w2[:, f, :], G[:, :, f, :], start=f == 0, stop=f == F - 1)
                last.then_inc(l3_ready, 1)

            def top1(u):
                pe.wait_ge(l3_copied, u + 1)
                pe.wait_ge(sum1_ready, (u + 1) * TILES)
                for m in range(N1 // P):
                    dst, ms = gbank[:, m * P:(m + 1) * P], slice(m * P, (m + 1) * P)
                    nc.tensor.matmul(dst, wt1[:, 0, ms], sum1[:, bass.ds(u * P, P)], start=True, stop=False)
                    nc.tensor.matmul(dst, wt1[:, 1, ms], G[:, :, F, :], start=False, stop=False)
                    nc.tensor.matmul(dst, wt1[:, 2, ms], sum3[:], start=False, stop=False)
                    last = nc.tensor.matmul(dst, wt1_dense[:, ms], dense[:, bass.ds(u * P, P)], start=False, stop=True)
                last.then_inc(h1_ready, 1)

            def top2(u):
                pe.wait_ge(h1_copied, u + 1)
                for m in range(N2 // P):
                    for k in range(N1 // P):
                        last = nc.tensor.matmul(gbank[:, m * P:(m + 1) * P], wt2[:, k, m * P:(m + 1) * P], h1[:, k, :],
                                                start=k == 0, stop=k == N1 // P - 1)
                last.then_inc(h2_ready, 1)

            def top3(u):
                pe.wait_ge(h2_copied, u + 1)
                for k in range(N2 // P):
                    last = nc.tensor.matmul(gbank[0:1, 0:P], wt3[:, k:k + 1], h2[:, k, :], start=k == 0,
                                            stop=k == N2 // P - 1)
                last.then_inc(y_ready, 1)

            pe.wait_ge(const_loaded, 3 * 16)
            transpose_rep(0, 0, 0)
            transpose_parts(0, 0)
            pe.wait_ge(sel_ready, 1)
            pe.wait_ge(w0_ready, 1)
            for k in range(PAIRK):
                select(0, k)
                sum_pairs(0, k)
            pe.wait_ge(w1_hi_ready, 1)
            pe.wait_ge(w1_lo_ready, 1)
            pe.wait_ge(top_loaded, 8 * 16)

            def quad(u, first, last):
                for i in range(TILES):
                    tile, more = u * TILES + i, not (last and i == TILES - 1)
                    nu, ni = (u, i + 1) if i < TILES - 1 else (u + 1, 0)
                    gs = g_slots(i)
                    pe.wait_ge(cur1_hi_ready, tile + 1)
                    pe.wait_ge(cur1_lo_ready, tile + 1)
                    for s in range(4 * PIECES):
                        n, q = 4 * i + s // PIECES, s % PIECES
                        layer2_piece(u, n, q)
                        if more and s == S_TA:
                            transpose_rep(tile + 1, nu, ni)
                        if more and s == S_TS:
                            transpose_parts(tile + 1, ni)
                        if more and s in S_SEL:
                            select(tile + 1, S_SEL.index(s))
                        if more and s in S_PAIR:
                            sum_pairs(tile + 1, S_PAIR.index(s))
                        if s in gs:
                            b = 4 * i + gs[s]
                            if b >= 0:
                                make_g(u, b)
                            elif not first:
                                make_g(u - 1, BLOCKS + b)
                        if i == 0 and not first:
                            if s == S_L3:
                                layer3(u - 1)
                            if s == S_H1:
                                top1(u - 1)
                            if s == S_H2:
                                top2(u - 1)
                            if s == S_Y:
                                top3(u - 1)

            over_quads(pe, quad)
            u = QUADS - 1
            make_g(u, BLOCKS - 2)
            make_g(u, BLOCKS - 1)
            layer3(u)
            top1(u)
            top2(u)
            top3(u)


def kernel(**inputs):
    import numpy as np
    import concourse.bacc as bacc
    from concourse.bass_utils import run_bass_kernel_spmd

    i = np.arange(F)
    w0 = np.asarray(inputs["L0_rec_f0"])
    rows = np.concatenate([i * F + (i + s) % F for s in SHIFTS])
    swapped = np.concatenate([(i + s) % F * F + i for s in SHIFTS[:-1]])

    sel = np.zeros((2, F, PAIRK * REP * F), np.float32)
    for n, s in enumerate(SHIFTS):
        sel[:, (i + s) % F, n * F + i] = 1.0
    blockmask = np.repeat(np.eye(BLK_B, dtype=np.float32), D, axis=0)

    def by_partition(v):
        return np.ascontiguousarray(np.asarray(v).reshape(-1, P).T)

    arrays = {
        "ids": np.asarray(inputs["ids"]),
        "w0": w0[rows], "w0_swapped": w0[swapped],
        "w1": np.asarray(inputs["L0_rec_f1"]), "w2": np.asarray(inputs["L0_rec_f2"]),
        "wt1": np.asarray(inputs["W_top1"]), "bt1": by_partition(inputs["b_top1"]),
        "wt2": np.asarray(inputs["W_top2"]), "bt2": by_partition(inputs["b_top2"]),
        "wt3": by_partition(inputs["W_top3"]),
        "dense": np.ascontiguousarray(np.asarray(inputs["dense_ctx"]).T),
        "ident": np.eye(P, dtype=np.float32), "blockmask": blockmask, "sel": sel.reshape(2 * F, -1),
    }
    for f in range(F):
        arrays[f"tbl_{f}"] = np.asarray(inputs[f"tbl_{f}"])

    nc = bacc.Bacc("TRN2", target_bir_lowering=False, num_devices=1)
    t = {k: nc.dram_tensor(f"in_{k}", v.shape, mybir.dt.from_np(v.dtype), kind="ExternalInput").ap()
         for k, v in arrays.items()}
    t["x_rows"] = nc.dram_tensor("x_rows", (B * D, ROW), FP32, kind="Internal").ap()
    out = nc.dram_tensor("out", (1, B), FP32, kind="ExternalOutput").ap()
    cin_kernel(nc, t, [t[f"tbl_{f}"] for f in range(F)], out)
    r = run_bass_kernel_spmd(nc, [{f"in_{k}": v for k, v in arrays.items()}], core_ids=[0])
    return r.results[0]["out"].reshape(B, 1)
```

```python
import concourse.bass as bass
from concourse import mybir
from contextlib import ExitStack

FP32 = mybir.dt.float32
F32R = mybir.dt.float32r
I32 = mybir.dt.int32
ALU = mybir.AluOpType
ACT = mybir.ActivationFunctionType
AX = mybir.AxisListType

B, F, D, H = 1024, 39, 16, 128
N1, N2, ND = 512, 256, 16
P = 128
BLK_B = P // D
TILE_B = 4 * BLK_B
QUADS = B // P
TILES, BLOCKS = 4, 16
COLS = 4 * P

REP = 3
ONE = REP * F
ROW = ONE + 1
FX = F + 1
KPART = REP * F

SHIFTS = F // 2 + 1
PAIRK = (SHIFTS + REP - 1) // REP
LAST_ROWS = (SHIFTS - REP * (PAIRK - 1)) * F
XT_ROWS = 2 * F

PIECES = 10
A_PIECES = [0, 2, 4, 6, 8]
D_PIECES = [1, 3, 5, 7, 9]
D_OPS = sum(min(4, F - 4 * q) for q in D_PIECES)
PARTS = 4 * len(A_PIECES)
TREE = 3
BANKS = 5

S_T = [14, 18, 30, 30]
S_PAIR = [3 + 4 * k for k in range(PAIRK)]
S_HIGH = [x + 1 for x in S_PAIR]
S_LOW = [x + 2 for x in S_PAIR]
S_SUM = [x + 7 for x in S_PAIR]
S_G = [2, 12, 22, 32]
S_G_FIRST = [2, 12, 22, 38]
L3_STEP = 3
S_L3 = range(24, 24 + F // L3_STEP)
S_L3_COPY = 37
S_H1 = range(40, 40 + N1 // P)
S_RELU1 = range(44, 46)
S_H2 = range(48, 48 + N2 // P)
S_RELU2 = 50
S_Y = 53
G_LAG = 3
Q_HALVE, Q_FINISH = 7, 8


def rows_of(k):
    return KPART if k < PAIRK - 1 else LAST_ROWS


GATHERS = 3
EARLY = 6
S_ROWS = [8, 10, 12]


def cin_kernel(nc, t, tables, out):
    ctx = ExitStack()
    with ctx:
        def sb(name, shape, dt=FP32):
            return ctx.enter_context(nc.sbuf_tensor(name, shape, dt))

        def bank(name):
            return ctx.enter_context(nc.psum_tensor(name, [P, 512], FP32))

        def sem(name):
            return ctx.enter_context(nc.semaphore(name))

        ident = sb("ident", [P, P])
        blockmask = sb("blockmask", [P, BLK_B])
        w0_hi = sb("w0_hi", [KPART, PAIRK, H], F32R)
        w0_lo = sb("w0_lo", [KPART, PAIRK, H], F32R)
        w1_hi = sb("w1_hi", [P, F * H], F32R)
        w1_lo = sb("w1_lo", [P, F * H], F32R)
        w2 = sb("w2", [P, F, H])
        wt1 = sb("wt1", [P, 3, N1])
        wt1_dense = sb("wt1_dense", [ND, N1])
        wt2 = sb("wt2", [P, N1 // P, N2])
        wt3 = sb("wt3", [P, N2 // P])
        bt1 = sb("bt1", [P, N1 // P])
        bt2 = sb("bt2", [P, N2 // P])
        dense = sb("dense", [ND, B])
        ids = sb("ids", [P, QUADS, F], I32)
        emb = sb("emb", [P, F, D])
        emb_rows = sb("emb_rows", [P, D, ROW])
        x_cols = [sb(f"x_cols{i}", [P, 4, ROW]) for i in range(TILES)]
        x_rep = [sb(f"x_rep{i}", [KPART, COLS]) for i in range(2)]
        partners = [sb(f"partners{i}", [KPART, PAIRK, COLS]) for i in range(2)]
        pairs = [sb(f"pairs{i}", [KPART, COLS]) for i in range(2)]
        pairs_hi = [sb(f"pairs_hi{i}", [KPART, COLS], F32R) for i in range(2)]
        pairs_lo = [sb(f"pairs_lo{i}", [KPART, COLS], F32R) for i in range(2)]
        cur1_hi = [sb(f"cur1_hi{i}", [P, COLS], F32R) for i in range(2)]
        cur1_lo = [sb(f"cur1_lo{i}", [P, COLS], F32R) for i in range(2)]
        parts = [sb(f"parts{i}", [P, PARTS, H]) for i in range(2)]
        tails = [sb(f"tails{i}", [P, 4, H]) for i in range(2)]
        cur2 = [sb(f"cur2_{i}", [P, H]) for i in range(2)]
        x_diag = [sb(f"x_diag{i}", [P, FX, BLK_B]) for i in range(2)]
        G = sb("G", [P, TILES, FX, TILE_B])
        sum1 = sb("sum1", [P, B])
        h1 = sb("h1", [P, N1 // P, P])
        h2 = sb("h2", [P, N2 // P, P])
        sum2, sum3 = h2[:, 0, :], h2[:, 1, :]
        y = sum1[0:1, :]
        pieces = [bank(f"pieces{i}") for i in range(BANKS)]
        xbank = bank("xbank")
        cur1_bank = bank("cur1_bank")
        gbank = bank("gbank")

        w0_raw = partners[1][:, 0:2, :].rearrange("p j c -> p (j c)")[:, 0:PAIRK * H].rearrange(
            "p (k m) -> p k m", m=H)
        w0_swapped = partners[1][:, 2:4, :].rearrange("p j c -> p (j c)")[:, 0:PAIRK * H].rearrange(
            "p (k m) -> p k m", m=H)
        w1_raw = [(parts[i][:, 0:n, :], slice(i * PARTS * H, (i * PARTS + n) * H))
                  for i, n in ((0, PARTS), (1, F - PARTS))]

        x_rows = t["x_rows"]
        x_wide = t["x_wide"]

        const_loaded = sem("const_loaded")
        w0_loaded = sem("w0_loaded")
        w1_loaded = sem("w1_loaded")
        top_loaded = sem("top_loaded")
        ids_loaded = sem("ids_loaded")
        zeros_set = sem("zeros_set")
        w0_summed = sem("w0_summed")
        w0_hi_ready = sem("w0_hi_ready")
        w0_lo_ready = sem("w0_lo_ready")
        w1_hi_ready = sem("w1_hi_ready")
        w1_lo_ready = sem("w1_lo_ready")
        gathered = sem("gathered")
        rows_copied = sem("rows_copied")
        rows_stored = sem("rows_stored")
        ones_set = sem("ones_set")
        x_loaded = [sem(f"x_loaded{i}") for i in range(TILES)]
        transposed = sem("transposed")
        x_rep_ready = sem("x_rep_ready")
        wide_stored = sem("wide_stored")
        partners_loaded = [sem(f"partners_loaded{i}") for i in range(2)]
        pairs_ready = sem("pairs_ready")
        pairs_hi_ready = sem("pairs_hi_ready")
        pairs_lo_ready = sem("pairs_lo_ready")
        pairs_used = sem("pairs_used")
        cur1_hi_ready = sem("cur1_hi_ready")
        cur1_lo_ready = sem("cur1_lo_ready")
        sum1_ready = sem("sum1_ready")
        l2d_ready = sem("l2d_ready")
        l2a_ready = sem("l2a_ready")
        acc_done = sem("acc_done")
        prod_done = sem("prod_done")
        tree_done = sem("tree_done")
        halved = sem("halved")
        cur2_ready = sem("cur2_ready")
        x_diag_ready = sem("x_diag_ready")
        g_ready = sem("g_ready")
        g_copied = sem("g_copied")
        l3_ready = sem("l3_ready")
        l3_copied = sem("l3_copied")
        h1_ready = sem("h1_ready")
        h1_copied = sem("h1_copied")
        h2_ready = sem("h2_ready")
        h2_copied = sem("h2_copied")
        y_ready = sem("y_ready")
        y_copied = sem("y_copied")
        out_stored = sem("out_stored")

        block = ctx.enter_context(nc.Block())

        def wait(eng, s, value):
            if not isinstance(value, int) or value > 0:
                eng.wait_ge(s, value)

        def value(eng, v):
            if not isinstance(v, int):
                eng.compute_val(v)
            return v

        def over_quads(eng, quad):
            quad(0, True, False)
            with eng.Fori(1, QUADS - 1) as u:
                quad(u, False, False)
            quad(QUADS - 1, False, True)

        @block.sync
        def _(sp):
            sp.dma_start(ids[:], t["ids"].rearrange("(u p) f -> p u f", p=P)).then_inc(ids_loaded, 16)
            for part, cols in w1_raw:
                sp.dma_start(part, t["w1"][cols, :].rearrange("(f g) m -> g f m", g=H)).then_inc(w1_loaded, 16)
            sp.dma_start(ident[:], t["ident"]).then_inc(const_loaded, 16)
            sp.dma_start(blockmask[:], t["blockmask"]).then_inc(const_loaded, 16)
            whole = KPART * (PAIRK - 1)
            sp.dma_start(w0_raw[:, 0:PAIRK - 1, :],
                         t["w0"][0:whole, :].rearrange("(k p) m -> p k m", p=KPART)).then_inc(w0_loaded, 16)
            sp.dma_start(w0_raw[0:LAST_ROWS, PAIRK - 1, :], t["w0"][whole:, :]).then_inc(w0_loaded, 16)
            sp.dma_start(w0_swapped[F:KPART, 0, :], t["w0_swapped"][0:KPART - F, :]).then_inc(w0_loaded, 16)
            sp.dma_start(w0_swapped[:, 1:PAIRK - 1, :], t["w0_swapped"][KPART - F:whole - F, :].rearrange(
                "(k p) m -> p k m", p=KPART)).then_inc(w0_loaded, 16)
            sp.dma_start(w0_swapped[0:LAST_ROWS, PAIRK - 1, :], t["w0_swapped"][whole - F:, :]
                         ).then_inc(w0_loaded, 16)
            sp.dma_start(w2[:], t["w2"].rearrange("(f g) m -> g f m", g=H)).then_inc(top_loaded, 16)
            sp.dma_start(wt1[:], t["wt1"][0:3 * P, :].rearrange("(k p) n -> p k n", p=P)).then_inc(top_loaded, 16)
            sp.dma_start(wt1_dense[:], t["wt1"][3 * P:3 * P + ND, :]).then_inc(top_loaded, 16)
            sp.dma_start(wt2[:], t["wt2"].rearrange("(k p) n -> p k n", p=P)).then_inc(top_loaded, 16)
            sp.dma_start(wt3[:], t["wt3"]).then_inc(top_loaded, 16)
            sp.dma_start(bt1[:], t["bt1"]).then_inc(top_loaded, 16)
            sp.dma_start(bt2[:], t["bt2"]).then_inc(top_loaded, 16)
            sp.dma_start(dense[:], t["dense"]).then_inc(top_loaded, 16)

            def store_rows(u):
                row, copied = value(sp, u * (P * D)), value(sp, u + 1)
                sp.wait_ge(rows_copied, copied)
                sp.dma_start(x_rows[bass.ds(row, P * D), :].rearrange("(b d) r -> b (d r)", d=D),
                             emb_rows[:].rearrange("p d r -> p (d r)")).then_inc(rows_stored, 16)

            def load_tile(u, i):
                row = value(sp, u * (P * D) + i * COLS)
                diag_used = value(sp, (u - 1) * BLOCKS + 4 * (i + 1))
                weighed = value(sp, ((u - 1) * BLOCKS + 4 * (i + 1)) * len(A_PIECES))
                stored = value(sp, (u + 1) * 16)
                wait(sp, x_diag_ready, diag_used)
                wait(sp, prod_done, weighed)
                wait(sp, rows_stored, stored)
                sp.dma_start(x_cols[i][:], x_rows[bass.ds(row, COLS), :].rearrange("(j c) r -> c j r", c=P)
                             ).then_inc(x_loaded[i], 16)

            def spread_tile(tile, i):
                copied, stored = value(sp, tile + 1), value(sp, (tile + 1) * 16)
                used = value(sp, (tile - 1) * PAIRK)
                sp.wait_ge(x_rep_ready, copied)
                sp.dma_start(x_wide[bass.ds(tile, 1), :, :].rearrange("o r c -> (o r) c"), x_rep[i % 2][0:XT_ROWS, :]
                             ).then_inc(wide_stored, 16)
                wait(sp, pairs_ready, used)
                sp.wait_ge(wide_stored, stored)
                for r in range(REP):
                    steps = len(range(r, SHIFTS, REP))
                    first = x_wide[bass.ds(tile, 1), r:r + F, :].rearrange("o r c -> (o r) c")
                    src = bass.AP(first.tensor, first.offset, [[COLS, F], [REP * COLS, steps], [1, COLS]])
                    sp.dma_start(partners[i % 2][r * F:(r + 1) * F, 0:steps, :], src
                                 ).then_inc(partners_loaded[i % 2], 16)

            store_rows(0)
            load_tile(0, 0)
            load_tile(0, 1)
            spread_tile(0, 0)
            sp.wait_ge(w0_lo_ready, 1)
            spread_tile(1, 1)

            def quad(u, first, last):
                load_tile(u, 2)
                spread_tile(u * TILES + 2, 2)
                load_tile(u, 3)
                spread_tile(u * TILES + 3, 3)
                if not last:
                    store_rows(u + 1)
                    load_tile(u + 1, 0)
                    load_tile(u + 1, 1)
                    spread_tile((u + 1) * TILES, 0)
                    spread_tile((u + 1) * TILES + 1, 1)

            over_quads(sp, quad)
            sp.wait_ge(y_copied, QUADS)
            sp.dma_start(out, y).then_inc(out_stored, 16)
            sp.wait_ge(out_stored, 16)

        @block.gpsimd
        def _(pool):
            def gather(u, f):
                pool.indirect_dma_start(
                    emb[:, f, :], None, tables[f],
                    bass.IndirectOffsetOnAxis(ap=next_ids[:, f:f + 1], axis=0)).then_inc(gathered, 16)

            def add_parts(u, n):
                g, v, out4 = u * BLOCKS + n, parts[n % 2], tails[n % 2]
                pool.wait_ge(prod_done, (g + 1) * len(A_PIECES))
                pool.wait_ge(acc_done, (g + 1) * D_OPS)
                pool.tensor_tensor(v[:, 0:8], v[:, 0:8], v[:, 8:16], ALU.add).then_inc(tree_done, 1)
                pool.wait_ge(tree_done, g * TREE + 1)
                pool.tensor_tensor(v[:, 0:4], v[:, 0:4], v[:, 4:8], ALU.add).then_inc(tree_done, 1)
                wait(pool, cur2_ready, g - 1)
                pool.wait_ge(tree_done, g * TREE + 2)
                pool.tensor_tensor(out4[:], v[:, 0:4], v[:, 16:20], ALU.add).then_inc(tree_done, 1)

            def make_x_diag(u, n):
                g = u * BLOCKS + n
                wait(pool, g_ready, g - 1)
                x = x_cols[n // 4][:, n % 4, ONE - F:ONE + 1]
                pool.tensor_tensor(x_diag[n % 2][:], x.unsqueeze(2).to_broadcast([P, FX, BLK_B]),
                                   blockmask[:].unsqueeze(1).to_broadcast([P, FX, BLK_B]), ALU.mult
                                   ).then_inc(x_diag_ready, 1)

            next_ids = sb("next_ids", [P, F], I32)
            ids_moved = sem("ids_moved")

            def move_ids(u):
                pool.tensor_copy(next_ids[:], ids[:, u, :]).then_inc(ids_moved, 1)
                pool.wait_ge(ids_moved, u + 1)

            pool.memset(emb_rows[:, :, ONE:ONE + 1], 1.0).then_inc(ones_set, 1)
            pool.wait_ge(ids_loaded, 16)
            move_ids(0)
            for f in range(F):
                gather(0, f)
            pool.wait_ge(gathered, F * 16)
            pool.wait_ge(rows_copied, 1)
            move_ids(1)
            for f in range(F):
                gather(1, f)

            def quad(u, first, last):
                for n in range(0 if first else -EARLY, BLOCKS - EARLY):
                    if not (first or last):
                        if n == -EARLY:
                            pool.wait_ge(gathered, (u + 1) * F * 16)
                            pool.wait_ge(rows_copied, u + 1)
                            move_ids(u + 1)
                        else:
                            start = GATHERS * (n + EARLY - 1)
                            for f in range(start, min(F, start + GATHERS)):
                                gather(u + 1, f)
                    add_parts(u, n)
                    make_x_diag(u, n)

            pool.wait_ge(const_loaded, 2 * 16)
            over_quads(pool, quad)
            for n in range(BLOCKS - EARLY, BLOCKS):
                add_parts(QUADS - 1, n)
                make_x_diag(QUADS - 1, n)

        @block.scalar
        def _(act):
            def copy_rows(u, r):
                if r == 0:
                    act.wait_ge(gathered, (u + 1) * F * 16)
                    wait(act, rows_stored, u * 16)
                last = nc.scalar.activation(emb_rows[:, :, r * F:(r + 1) * F], emb[:].rearrange("p f d -> p d f"),
                                            ACT.Copy)
                if r == REP - 1:
                    last.then_inc(rows_copied, 1)

            def weigh_piece(u, n, q):
                g, i = u * BLOCKS + n, A_PIECES.index(q)
                k = g * len(A_PIECES) + i
                if i == 0:
                    wait(act, tree_done, (g - 1) * TREE)
                    act.wait_ge(x_loaded[n // 4], (u + 1) * 16)
                act.wait_ge(l2a_ready, k + 1)
                src = pieces[(n * PIECES + q) % BANKS]
                for r in range(4):
                    f = 4 * q + r
                    last = nc.scalar.activation(parts[n % 2][:, 4 * i + r, :], src[:, r * H:(r + 1) * H], ACT.Copy,
                                                scale=x_cols[n // 4][:, n % 4, f:f + 1])
                last.then_inc(prod_done, 1)

            def copy_x_rep(tile, i):
                act.wait_ge(transposed, tile + 1)
                wait(act, pairs_ready, (tile - 1) * PAIRK)
                wait(act, wide_stored, (tile - 1) * 16)
                nc.scalar.activation(x_rep[i % 2][:], xbank[0:KPART, :], ACT.Copy).then_inc(x_rep_ready, 1)

            def take_pairs_high(tile, i, k):
                g, buf, rows = tile * PAIRK + k, (i * PAIRK + k) % 2, rows_of(k)
                act.wait_ge(pairs_ready, g + 1)
                wait(act, pairs_used, g - 1)
                nc.scalar.activation(pairs_hi[buf][0:rows, :], pairs[buf][0:rows, :], ACT.Copy
                                     ).then_inc(pairs_hi_ready, 1)

            def copy_cur1_hi(tile, i):
                act.wait_ge(pairs_used, (tile + 1) * PAIRK)
                wait(act, l2d_ready, (tile - 1) * 4 * len(D_PIECES))
                nc.scalar.activation(cur1_hi[i % 2][:], cur1_bank[:], ACT.Copy).then_inc(cur1_hi_ready, 1)

            def copy_g(u, n):
                g = u * BLOCKS + n
                act.wait_ge(g_ready, g + 1)
                if n == 0:
                    wait(act, l3_copied, u)
                dst = G[:, n // 4, :, (n % 4) * BLK_B:(n % 4 + 1) * BLK_B]
                nc.scalar.activation(dst, gbank[:, 0:FX * BLK_B].rearrange("p (f b) -> p f b", b=BLK_B),
                                     ACT.Copy).then_inc(g_copied, 1)

            def copy_l3(u):
                act.wait_ge(l3_ready, u + 1)
                wait(act, y_ready, u)
                nc.scalar.activation(sum2.rearrange("p (t b) -> p t b", b=TILE_B), G[:, :, F, :], ACT.Copy)
                nc.scalar.activation(sum3, xbank[:, 0:P], ACT.Copy).then_inc(l3_copied, 1)

            def relu1(u, half):
                act.wait_ge(h1_ready, u + 1)
                wait(act, h2_ready, u)
                for m in range(half * N1 // P // 2, (half + 1) * N1 // P // 2):
                    last = nc.scalar.activation(h1[:, m, :], xbank[:, m * P:(m + 1) * P], ACT.Relu,
                                                bias=bt1[:, m:m + 1])
                last.then_inc(h1_copied, 1)

            def relu2(u):
                act.wait_ge(h2_ready, u + 1)
                act.wait_ge(h1_ready, u + 1)
                for m in range(N2 // P):
                    last = nc.scalar.activation(h2[:, m, :], xbank[:, m * P:(m + 1) * P], ACT.Relu,
                                                bias=bt2[:, m:m + 1])
                last.then_inc(h2_copied, 1)

            def copy_y(u):
                act.wait_ge(y_ready, u + 1)
                nc.scalar.activation(sum1[0:1, bass.ds(u * P, P)], xbank[0:1, 0:P], ACT.Copy).then_inc(y_copied, 1)

            act.wait_ge(w1_loaded, 2 * 16)
            for part, cols in w1_raw:
                last = nc.scalar.activation(w1_hi[:, cols], part.rearrange("p f m -> p (f m)"), ACT.Copy)
            last.then_inc(w1_hi_ready, 1)
            act.wait_ge(w0_summed, 1)
            nc.scalar.activation(w0_hi[:, 0:PAIRK - 1, :], w0_raw[:, 0:PAIRK - 1, :], ACT.Copy)
            nc.scalar.activation(w0_hi[0:LAST_ROWS, PAIRK - 1, :], w0_raw[0:LAST_ROWS, PAIRK - 1, :], ACT.Copy
                                 ).then_inc(w0_hi_ready, 1)
            act.wait_ge(ones_set, 1)
            for r in range(REP):
                copy_rows(0, r)
            copy_x_rep(0, 0)
            copy_x_rep(1, 1)
            for k in range(PAIRK):
                take_pairs_high(0, 0, k)
            copy_cur1_hi(0, 0)
            act.wait_ge(w1_lo_ready, 1)
            act.wait_ge(top_loaded, 8 * 16)

            def quad(u, first, last):
                for i in range(TILES):
                    tile, more = u * TILES + i, not (last and i == TILES - 1)
                    for s in range(4 * PIECES):
                        n, q = 4 * i + s // PIECES, s % PIECES
                        if q in A_PIECES:
                            weigh_piece(u, n, q)
                        if more and s in S_HIGH:
                            take_pairs_high(tile + 1, i + 1, S_HIGH.index(s))
                        if s == S_T[i] + 1 and not (last and i >= TILES - 2):
                            copy_x_rep(tile + 2, i + 2)
                        if s - 1 in (S_G_FIRST if i == 0 else S_G):
                            if n >= G_LAG:
                                copy_g(u, n - G_LAG)
                            elif not first:
                                copy_g(u - 1, BLOCKS + n - G_LAG)
                        at = 4 * PIECES * i + s
                        if not first:
                            if at == S_L3_COPY:
                                copy_l3(u - 1)
                            if at in S_RELU1:
                                relu1(u - 1, S_RELU1.index(at))
                            if at == S_RELU2:
                                relu2(u - 1)
                            if at - 1 == S_Y:
                                copy_y(u - 1)
                        if i == 2 and s in S_ROWS and not last:
                            copy_rows(u + 1, S_ROWS.index(s))
                        if more and s == S_SUM[-1] + 1:
                            copy_cur1_hi(tile + 1, i + 1)

            over_quads(act, quad)
            u = QUADS - 1
            for n in range(BLOCKS - G_LAG, BLOCKS):
                copy_g(u, n)
            copy_l3(u)
            relu1(u, 0)
            relu1(u, 1)
            relu2(u)
            copy_y(u)

        @block.vector
        def _(dve):
            def sum_piece(u, n, q):
                g, i = u * BLOCKS + n, D_PIECES.index(q)
                if i == 0:
                    dve.wait_ge(prod_done, g * len(A_PIECES) + 1)
                dve.wait_ge(l2d_ready, g * len(D_PIECES) + i + 1)
                src = pieces[(n * PIECES + q) % BANKS]
                for r in range(min(4, F - 4 * q)):
                    f, e = 4 * q + r, 4 * i + r
                    acc = parts[n % 2][:, r, :]
                    if i > 0 and r % 2 == 0:
                        dve.wait_ge(acc_done, g * D_OPS + min(e - 2, D_OPS))
                    nc.vector.scalar_tensor_tensor(acc, src[:, r * H:(r + 1) * H], x_cols[n // 4][:, n % 4, f:f + 1],
                                                   acc, ALU.mult, ALU.add).then_inc(acc_done, 1)

            def make_pairs(tile, i, k):
                g, buf, rows = tile * PAIRK + k, (i * PAIRK + k) % 2, rows_of(k)
                if k == 0:
                    dve.wait_ge(x_rep_ready, tile + 1)
                    dve.wait_ge(partners_loaded[i % 2], ((tile - i % 2) * 8 + 16) * REP)
                wait(dve, pairs_lo_ready, g - 1)
                nc.vector.tensor_tensor(pairs[buf][0:rows, :], partners[i % 2][0:rows, k, :], x_rep[i % 2][0:rows, :],
                                        ALU.mult).then_inc(pairs_ready, 1)

            def take_pairs_low(tile, i, k):
                g, buf, rows = tile * PAIRK + k, (i * PAIRK + k) % 2, rows_of(k)
                dve.wait_ge(pairs_hi_ready, g + 1)
                wait(dve, pairs_used, g - 1)
                nc.vector.tensor_tensor(pairs_lo[buf][0:rows, :], pairs[buf][0:rows, :],
                                        pairs_hi[buf][0:rows, :].bitcast(FP32), ALU.subtract
                                        ).then_inc(pairs_lo_ready, 1)

            def take_cur1(tile, col, i):
                dve.wait_ge(cur1_hi_ready, tile + 1)
                nc.vector.tensor_tensor(cur1_lo[i % 2][:], cur1_bank[:], cur1_hi[i % 2][:].bitcast(FP32),
                                        ALU.subtract).then_inc(cur1_lo_ready, 1)
                nc.vector.tensor_reduce(sum1[:, bass.ds(col, TILE_B)],
                                        cur1_bank[:].rearrange("p (b d) -> p b d", d=D), AX.X, ALU.add
                                        ).then_inc(sum1_ready, 1)

            def halve_tails(u, n):
                g, v = u * BLOCKS + n, tails[n % 2]
                dve.wait_ge(tree_done, (g + 1) * TREE)
                nc.vector.tensor_tensor(v[:, 0:2], v[:, 0:2], v[:, 2:4], ALU.add).then_inc(halved, 1)

            def finish_cur2(u, n):
                g, v = u * BLOCKS + n, tails[n % 2]
                wait(dve, g_ready, g - 1)
                dve.wait_ge(halved, g + 1)
                nc.vector.tensor_tensor(cur2[n % 2][:], v[:, 0], v[:, 1], ALU.add).then_inc(cur2_ready, 1)

            nc.vector.memset(w0_swapped[0:F, 0, :], 0.0).then_inc(zeros_set, 1)
            dve.wait_ge(w0_loaded, 5 * 16)
            dve.wait_ge(zeros_set, 1)
            for rows, ks in ((KPART, slice(0, PAIRK - 1)), (LAST_ROWS, slice(PAIRK - 1, PAIRK))):
                last = nc.vector.tensor_tensor(w0_raw[0:rows, ks, :], w0_raw[0:rows, ks, :], w0_swapped[0:rows, ks, :],
                                               ALU.add)
            last.then_inc(w0_summed, 1)
            dve.wait_ge(w0_hi_ready, 1)
            for rows, ks in ((KPART, slice(0, PAIRK - 1)), (LAST_ROWS, slice(PAIRK - 1, PAIRK))):
                last = nc.vector.tensor_tensor(w0_lo[0:rows, ks, :], w0_raw[0:rows, ks, :],
                                               w0_hi[0:rows, ks, :].bitcast(FP32), ALU.subtract)
            last.then_inc(w0_lo_ready, 1)
            dve.wait_ge(w1_hi_ready, 1)
            for part, cols in w1_raw:
                last = nc.vector.tensor_tensor(w1_lo[:, cols], part.rearrange("p f m -> p (f m)"),
                                               w1_hi[:, cols].bitcast(FP32), ALU.subtract)
            last.then_inc(w1_lo_ready, 1)
            make_pairs(0, 0, 0)
            for k in range(1, PAIRK):
                make_pairs(0, 0, k)
                take_pairs_low(0, 0, k - 1)
            take_pairs_low(0, 0, PAIRK - 1)
            take_cur1(0, 0, 0)

            def quad(u, first, last):
                for i in range(TILES):
                    tile, more = u * TILES + i, not (last and i == TILES - 1)
                    for s in range(4 * PIECES):
                        n, q = 4 * i + s // PIECES, s % PIECES
                        if q in D_PIECES:
                            sum_piece(u, n, q)
                        if q in (Q_HALVE, Q_FINISH):
                            step = halve_tails if q == Q_HALVE else finish_cur2
                            if n >= 2:
                                step(u, n - 2)
                            elif not first:
                                step(u - 1, BLOCKS + n - 2)
                        if more and s in S_PAIR:
                            make_pairs(tile + 1, i + 1, S_PAIR.index(s))
                        if more and s in S_LOW:
                            take_pairs_low(tile + 1, i + 1, S_LOW.index(s))
                        if more and s == S_SUM[-1] + 2:
                            take_cur1(tile + 1, (tile + 1) * TILE_B, i + 1)

            over_quads(dve, quad)
            for n in (BLOCKS - 2, BLOCKS - 1):
                halve_tails(QUADS - 1, n)
                finish_cur2(QUADS - 1, n)

        @block.tensor
        def _(pe):
            def transpose_x(tile, u, i, first=True):
                pe.wait_ge(x_loaded[i], (u + 1) * 16)
                wait(pe, x_rep_ready, tile)
                if i == 3 and not first:
                    pe.wait_ge(y_copied, u)
                for j in range(4):
                    last = nc.tensor.transpose(xbank[0:KPART, j * P:(j + 1) * P], x_cols[i][:, j, 0:KPART], ident[:])
                last.then_inc(transposed, 1)

            def sum_pairs(tile, i, k):
                g, buf, rows = tile * PAIRK + k, (i * PAIRK + k) % 2, rows_of(k)
                pe.wait_ge(pairs_lo_ready, g + 1)
                if k == 0:
                    wait(pe, cur1_lo_ready, tile)
                    wait(pe, sum1_ready, tile)
                hi, lo = pairs_hi[buf][0:rows, :], pairs_lo[buf][0:rows, :]
                nc.tensor.matmul(cur1_bank[:], w0_hi[0:rows, k, :], hi, start=k == 0, stop=False)
                nc.tensor.matmul(cur1_bank[:], w0_lo[0:rows, k, :], hi, start=False, stop=False)
                nc.tensor.matmul(cur1_bank[:], w0_hi[0:rows, k, :], lo, start=False, stop=k == PAIRK - 1
                                 ).then_inc(pairs_used, 1)

            def layer2_piece(u, n, q):
                width = min(4, F - 4 * q) * H
                dst = pieces[(n * PIECES + q) % BANKS]
                g, back = (u * BLOCKS + n, q - BANKS) if q >= BANKS else (u * BLOCKS + n - 1, q - BANKS + PIECES)
                if back in D_PIECES:
                    wait(pe, acc_done, g * D_OPS + min(4 * (D_PIECES.index(back) + 1), D_OPS))
                else:
                    wait(pe, prod_done, g * len(A_PIECES) + A_PIECES.index(back) + 1)
                lo, hi = cur1_lo[n // 4 % 2], cur1_hi[n // 4 % 2]
                cols = slice(n % 4 * P, (n % 4 + 1) * P)
                ws = slice(4 * q * H, 4 * q * H + width)
                nc.tensor.matmul(dst[:, 0:width], hi[:, cols], w1_hi[:, ws], start=True, stop=False)
                nc.tensor.matmul(dst[:, 0:width], hi[:, cols], w1_lo[:, ws], start=False, stop=False)
                nc.tensor.matmul(dst[:, 0:width], lo[:, cols], w1_hi[:, ws], start=False, stop=True
                                 ).then_inc(l2d_ready if q in D_PIECES else l2a_ready, 1)

            def make_g(u, n):
                g = u * BLOCKS + n
                pe.wait_ge(cur2_ready, g + 1)
                pe.wait_ge(x_diag_ready, g + 1)
                wait(pe, g_copied, g)
                nc.tensor.matmul(gbank[:, 0:FX * BLK_B], cur2[n % 2][:], x_diag[n % 2][:].rearrange("p f b -> p (f b)"),
                                 start=True, stop=True).then_inc(g_ready, 1)

            def layer3(u, step, tiles):
                if step == 0:
                    pe.wait_ge(g_copied, (u + 1) * BLOCKS)
                    pe.wait_ge(x_rep_ready, tiles)
                for f in range(step * L3_STEP, (step + 1) * L3_STEP):
                    last = nc.tensor.matmul(xbank[:, 0:P], w2[:, f, :], G[:, :, f, :], start=f == 0, stop=f == F - 1)
                if step == F // L3_STEP - 1:
                    last.then_inc(l3_ready, 1)

            def top1(u, m):
                dst, ms = xbank[:, m * P:(m + 1) * P], slice(m * P, (m + 1) * P)
                if m == 0:
                    pe.wait_ge(sum1_ready, (u + 1) * TILES)
                    pe.wait_ge(l3_copied, u + 1)
                nc.tensor.matmul(dst, wt1[:, 0, ms], sum1[:, bass.ds(u * P, P)], start=True, stop=False)
                nc.tensor.matmul(dst, wt1_dense[:, ms], dense[:, bass.ds(u * P, P)], start=False, stop=False)
                nc.tensor.matmul(dst, wt1[:, 1, ms], sum2, start=False, stop=False)
                last = nc.tensor.matmul(dst, wt1[:, 2, ms], sum3, start=False, stop=True)
                if m == N1 // P - 1:
                    last.then_inc(h1_ready, 1)

            def top2(u, m):
                pe.wait_ge(h1_copied, (u + 1) * 2)
                for k in range(N1 // P):
                    last = nc.tensor.matmul(xbank[:, m * P:(m + 1) * P], wt2[:, k, m * P:(m + 1) * P], h1[:, k, :],
                                            start=k == 0, stop=k == N1 // P - 1)
                if m == N2 // P - 1:
                    last.then_inc(h2_ready, 1)

            def top3(u):
                pe.wait_ge(h2_copied, u + 1)
                for k in range(N2 // P):
                    last = nc.tensor.matmul(xbank[0:1, 0:P], wt3[:, k:k + 1], h2[:, k, :], start=k == 0,
                                            stop=k == N2 // P - 1)
                last.then_inc(y_ready, 1)

            pe.wait_ge(const_loaded, 2 * 16)
            transpose_x(0, 0, 0)
            transpose_x(1, 0, 1)
            pe.wait_ge(w0_hi_ready, 1)
            pe.wait_ge(w0_lo_ready, 1)
            for k in range(PAIRK):
                sum_pairs(0, 0, k)
            pe.wait_ge(w1_hi_ready, 1)
            pe.wait_ge(w1_lo_ready, 1)
            pe.wait_ge(top_loaded, 8 * 16)

            def quad(u, first, last):
                for i in range(TILES):
                    tile, more = u * TILES + i, not (last and i == TILES - 1)
                    nu, ni = (u, i + 2) if i < TILES - 2 else (u + 1, i + 2 - TILES)
                    pe.wait_ge(cur1_hi_ready, tile + 1)
                    pe.wait_ge(cur1_lo_ready, tile + 1)
                    for s in range(4 * PIECES):
                        n, q = 4 * i + s // PIECES, s % PIECES
                        layer2_piece(u, n, q)
                        if s == S_T[i] and not (last and i >= TILES - 2):
                            transpose_x(tile + 2, nu, ni, first)
                        if more and s in S_SUM:
                            sum_pairs(tile + 1, i + 1, S_SUM.index(s))
                        if s in (S_G_FIRST if i == 0 else S_G):
                            if n >= G_LAG:
                                make_g(u, n - G_LAG)
                            elif not first:
                                make_g(u - 1, BLOCKS + n - G_LAG)
                        at = 4 * PIECES * i + s
                        if not first:
                            if at in S_L3:
                                layer3(u - 1, S_L3.index(at), u * TILES + 3)
                            if at in S_H1:
                                top1(u - 1, S_H1.index(at))
                            if at in S_H2:
                                top2(u - 1, S_H2.index(at))
                            if at == S_Y:
                                top3(u - 1)

            over_quads(pe, quad)
            u = QUADS - 1
            for n in range(BLOCKS - G_LAG, BLOCKS):
                make_g(u, n)
            for step in range(F // L3_STEP):
                layer3(u, step, QUADS * TILES)
            for m in range(N1 // P):
                top1(u, m)
            for m in range(N2 // P):
                top2(u, m)
            top3(u)


def kernel(**inputs):
    import numpy as np
    import concourse.bacc as bacc
    from concourse.bass_utils import run_bass_kernel_spmd

    i = np.arange(F)
    w0 = np.asarray(inputs["L0_rec_f0"])
    rows = np.concatenate([i * F + (i + s) % F for s in range(SHIFTS)])
    swapped = np.concatenate([(i + s) % F * F + i for s in range(1, SHIFTS)])

    blockmask = np.repeat(np.eye(BLK_B, dtype=np.float32), D, axis=0)

    def by_partition(v):
        return np.ascontiguousarray(np.asarray(v).reshape(-1, P).T)

    arrays = {
        "ids": np.asarray(inputs["ids"]),
        "w0": w0[rows], "w0_swapped": w0[swapped],
        "w1": np.asarray(inputs["L0_rec_f1"]), "w2": np.asarray(inputs["L0_rec_f2"]),
        "wt1": np.asarray(inputs["W_top1"]), "bt1": by_partition(inputs["b_top1"]),
        "wt2": np.asarray(inputs["W_top2"]), "bt2": by_partition(inputs["b_top2"]),
        "wt3": by_partition(inputs["W_top3"]),
        "dense": np.ascontiguousarray(np.asarray(inputs["dense_ctx"]).T),
        "ident": np.eye(P, dtype=np.float32), "blockmask": blockmask,
    }
    for f in range(F):
        arrays[f"tbl_{f}"] = np.asarray(inputs[f"tbl_{f}"])

    nc = bacc.Bacc("TRN2", target_bir_lowering=False, num_devices=1)
    t = {k: nc.dram_tensor(f"in_{k}", v.shape, mybir.dt.from_np(v.dtype), kind="ExternalInput").ap()
         for k, v in arrays.items()}
    t["x_rows"] = nc.dram_tensor("x_rows", (B * D, ROW), FP32, kind="Internal").ap()
    t["x_wide"] = nc.dram_tensor("x_wide", (B // TILE_B, XT_ROWS, COLS), FP32, kind="Internal").ap()
    out = nc.dram_tensor("out", (1, B), FP32, kind="ExternalOutput").ap()
    cin_kernel(nc, t, [t[f"tbl_{f}"] for f in range(F)], out)
    r = run_bass_kernel_spmd(nc, [{f"in_{k}": v for k, v in arrays.items()}], core_ids=[0])
    return r.results[0]["out"].reshape(B, 1)
```

```python
import concourse.bass as bass
from concourse import mybir
from contextlib import ExitStack

FP32 = mybir.dt.float32
F32R = mybir.dt.float32r
I32 = mybir.dt.int32
ALU = mybir.AluOpType
ACT = mybir.ActivationFunctionType
AX = mybir.AxisListType

B, F, D, H = 1024, 39, 16, 128
N1, N2, ND = 512, 256, 16
P = 128
BLK_B = P // D
TILE_B = 4 * BLK_B
QUADS = B // P
TILES, BLOCKS = 4, 16
COLS = 4 * P

REP = 3
ONE = REP * F
ROW = ONE + 1
FX = F + 1
KPART = REP * F

SHIFTS = F // 2 + 1
PAIRK = (SHIFTS + REP - 1) // REP
LAST_ROWS = (SHIFTS - REP * (PAIRK - 1)) * F
XT_ROWS = 2 * F

PIECES = 10
A_PIECES = [0, 2, 4, 6, 8]
D_PIECES = [1, 3, 5, 7, 9]
D_OPS = sum(min(4, F - 4 * q) for q in D_PIECES)
PARTS = 4 * len(A_PIECES)
WARM_UP = 14
TREE = 3
BANKS = 5

S_T = [14, 20, 30, 20]
S_PAIR = [3 + 4 * k for k in range(PAIRK)]
S_HIGH = [x + 1 for x in S_PAIR]
S_LOW = [x + 2 for x in S_PAIR]
S_SUM = [x + 7 for x in S_PAIR]
S_G = [2, 12, 22, 32]
S_G_FIRST = [2, 12, 22, 38]
L3_STEP = 3
S_L3 = range(25, 25 + F // L3_STEP)
S_L3_COPY = 38
S_H1 = range(41, 41 + N1 // P)
S_RELU1 = range(45, 47)
S_H2 = range(50, 50 + N2 // P)
S_RELU2 = 52
S_Y = 55
G_LAG = 3
Q_HALVE, Q_FINISH = 7, 8


GATHER_BLOCKS = 14
EARLY = 7
AHEAD = 27
S_ROWS = [7, 11, 15]


def rows_of(k):
    return KPART if k < PAIRK - 1 else LAST_ROWS


def cin_kernel(nc, t, tables, out):
    ctx = ExitStack()
    with ctx:
        def sb(name, shape, dt=FP32):
            return ctx.enter_context(nc.sbuf_tensor(name, shape, dt))

        def bank(name):
            return ctx.enter_context(nc.psum_tensor(name, [P, 512], FP32))

        def sem(name):
            return ctx.enter_context(nc.semaphore(name))

        ident = sb("ident", [P, P])
        blockmask = sb("blockmask", [P, BLK_B])
        w0_hi = sb("w0_hi", [KPART, PAIRK, H], F32R)
        w0_lo = sb("w0_lo", [KPART, PAIRK, H], F32R)
        w1_hi = sb("w1_hi", [P, F * H], F32R)
        w1_lo = sb("w1_lo", [P, F * H], F32R)
        w2 = sb("w2", [P, F, H])
        wt1 = sb("wt1", [P, 3, N1])
        wt1_dense = sb("wt1_dense", [ND, N1])
        wt2 = sb("wt2", [P, N1 // P, N2])
        wt3 = sb("wt3", [P, N2 // P])
        bt1 = sb("bt1", [P, N1 // P])
        bt2 = sb("bt2", [P, N2 // P])
        dense = sb("dense", [ND, B])
        ids = sb("ids", [P, QUADS, F], I32)
        emb = sb("emb", [P, F, D])
        emb_rows = sb("emb_rows", [P, D, ROW])
        x_cols = [sb(f"x_cols{i}", [P, 4, ROW]) for i in range(TILES)]
        x_rep = [sb(f"x_rep{i}", [KPART, COLS]) for i in range(2)]
        partners = [sb(f"partners{i}", [KPART, PAIRK, COLS]) for i in range(2)]
        pairs = [sb(f"pairs{i}", [KPART, COLS]) for i in range(2)]
        pairs_hi = [sb(f"pairs_hi{i}", [KPART, COLS], F32R) for i in range(2)]
        pairs_lo = [sb(f"pairs_lo{i}", [KPART, COLS], F32R) for i in range(2)]
        cur1_hi = [sb(f"cur1_hi{i}", [P, COLS], F32R) for i in range(2)]
        cur1_lo = [sb(f"cur1_lo{i}", [P, COLS], F32R) for i in range(2)]
        parts = [sb(f"parts{i}", [P, PARTS, H]) for i in range(2)]
        tails = [sb(f"tails{i}", [P, 4, H]) for i in range(2)]
        cur2 = [sb(f"cur2_{i}", [P, H]) for i in range(2)]
        x_diag = [sb(f"x_diag{i}", [P, FX, BLK_B]) for i in range(2)]
        G = sb("G", [P, TILES, FX, TILE_B])
        sum1 = sb("sum1", [P, B])
        h1 = sb("h1", [P, N1 // P, P])
        h2 = sb("h2", [P, N2 // P, P])
        sum2, sum3 = h2[:, 0, :], h2[:, 1, :]
        y = sum1[0:1, :]
        pieces = [bank(f"pieces{i}") for i in range(BANKS)]
        xbank = bank("xbank")
        cur1_bank = bank("cur1_bank")
        gbank = bank("gbank")

        h_sums = [xbank[:, m * P:(m + 1) * P] for m in range(N1 // P)]
        h1_last = [pieces[m][:, 0:P] for m in range(N1 // P)]
        h2_last = [pieces[4][:, m * P:(m + 1) * P] for m in range(N2 // P)]

        w0_raw = partners[1][:, 0:2, :].rearrange("p j c -> p (j c)")[:, 0:PAIRK * H].rearrange(
            "p (k m) -> p k m", m=H)
        w0_swapped = partners[1][:, 2:4, :].rearrange("p j c -> p (j c)")[:, 0:PAIRK * H].rearrange(
            "p (k m) -> p k m", m=H)
        w1_raw = [(parts[i][:, 0:n, :], slice(i * PARTS * H, (i * PARTS + n) * H))
                  for i, n in ((0, PARTS), (1, F - PARTS))]

        shift_rows = G[0:F].rearrange("p t f b -> p (t f b)")[:, 0:PAIRK * KPART].rearrange(
            "p (k r) -> p k r", r=KPART)

        x_wide = t["x_wide"]

        const_loaded = sem("const_loaded")
        w0_loaded = sem("w0_loaded")
        w1_loaded = sem("w1_loaded")
        top_loaded = sem("top_loaded")
        ids_loaded = sem("ids_loaded")
        zeros_set = sem("zeros_set")
        w0_summed = sem("w0_summed")
        w0_hi_ready = sem("w0_hi_ready")
        w0_lo_ready = sem("w0_lo_ready")
        w1_hi_ready = sem("w1_hi_ready")
        w1_lo_ready = sem("w1_lo_ready")
        gathered = sem("gathered")
        rows_copied = sem("rows_copied")
        ones_set = sem("ones_set")
        x_loaded = [sem(f"x_loaded{i}") for i in range(TILES)]
        transposed = sem("transposed")
        x_rep_ready = sem("x_rep_ready")
        first_partners = sem("first_partners")
        wide_stored = sem("wide_stored")
        partners_loaded = [sem(f"partners_loaded{i}") for i in range(2)]
        pairs_ready = sem("pairs_ready")
        pairs_hi_ready = sem("pairs_hi_ready")
        pairs_lo_ready = sem("pairs_lo_ready")
        pairs_used = sem("pairs_used")
        cur1_hi_ready = sem("cur1_hi_ready")
        cur1_lo_ready = sem("cur1_lo_ready")
        sum1_ready = sem("sum1_ready")
        l2d_ready = sem("l2d_ready")
        l2a_ready = sem("l2a_ready")
        acc_done = sem("acc_done")
        prod_done = sem("prod_done")
        tree_done = sem("tree_done")
        halved = sem("halved")
        cur2_ready = sem("cur2_ready")
        x_diag_ready = sem("x_diag_ready")
        g_ready = sem("g_ready")
        g_copied = sem("g_copied")
        l3_ready = sem("l3_ready")
        l3_copied = sem("l3_copied")
        h1_ready = sem("h1_ready")
        h1_copied = sem("h1_copied")
        h2_ready = sem("h2_ready")
        h2_copied = sem("h2_copied")
        y_ready = sem("y_ready")
        y_copied = sem("y_copied")
        out_stored = sem("out_stored")

        block = ctx.enter_context(nc.Block())

        def wait(eng, s, value):
            if not isinstance(value, int) or value > 0:
                eng.wait_ge(s, value)

        def value(eng, v):
            if not isinstance(v, int):
                eng.compute_val(v)
            return v

        def over_quads(eng, quad):
            quad(0, True, False)
            with eng.Fori(1, QUADS - 1) as u:
                quad(u, False, False)
            quad(QUADS - 1, False, True)

        @block.sync
        def _(sp):
            sp.dma_start(ids[:], t["ids"].rearrange("(u p) f -> p u f", p=P)).then_inc(ids_loaded, 16)
            for part, cols in w1_raw:
                sp.dma_start(part, t["w1"][cols, :].rearrange("(f g) m -> g f m", g=H)).then_inc(w1_loaded, 16)
            sp.dma_start(ident[:], t["ident"]).then_inc(const_loaded, 16)
            sp.dma_start(blockmask[:], t["blockmask"]).then_inc(const_loaded, 16)
            sp.dma_start(shift_rows, t["shift_rows"]).then_inc(const_loaded, 16)
            whole = KPART * (PAIRK - 1)
            sp.dma_start(w0_raw[:, 0:PAIRK - 1, :],
                         t["w0"][0:whole, :].rearrange("(k p) m -> p k m", p=KPART)).then_inc(w0_loaded, 16)
            sp.dma_start(w0_raw[0:LAST_ROWS, PAIRK - 1, :], t["w0"][whole:, :]).then_inc(w0_loaded, 16)
            sp.dma_start(w0_swapped[F:KPART, 0, :], t["w0_swapped"][0:KPART - F, :]).then_inc(w0_loaded, 16)
            sp.dma_start(w0_swapped[:, 1:PAIRK - 1, :], t["w0_swapped"][KPART - F:whole - F, :].rearrange(
                "(k p) m -> p k m", p=KPART)).then_inc(w0_loaded, 16)
            sp.dma_start(w0_swapped[0:LAST_ROWS, PAIRK - 1, :], t["w0_swapped"][whole - F:, :]
                         ).then_inc(w0_loaded, 16)
            sp.dma_start(w2[:], t["w2"].rearrange("(f g) m -> g f m", g=H)).then_inc(top_loaded, 16)
            sp.dma_start(wt1[:], t["wt1"][0:3 * P, :].rearrange("(k p) n -> p k n", p=P)).then_inc(top_loaded, 16)
            sp.dma_start(wt1_dense[:], t["wt1"][3 * P:3 * P + ND, :]).then_inc(top_loaded, 16)
            sp.dma_start(wt2[:], t["wt2"].rearrange("(k p) n -> p k n", p=P)).then_inc(top_loaded, 16)
            sp.dma_start(wt3[:], t["wt3"]).then_inc(top_loaded, 16)
            sp.dma_start(bt1[:], t["bt1"]).then_inc(top_loaded, 16)
            sp.dma_start(bt2[:], t["bt2"]).then_inc(top_loaded, 16)
            sp.dma_start(dense[:], t["dense"]).then_inc(top_loaded, 16)

            def load_tile(u, i):
                copied = value(sp, u + 1)
                diag_used = value(sp, (u - 1) * BLOCKS + 4 * (i + 1))
                weighed = value(sp, ((u - 1) * BLOCKS + 4 * (i + 1)) * len(A_PIECES))
                wait(sp, x_diag_ready, diag_used)
                wait(sp, prod_done, weighed)
                wait(sp, rows_copied, copied)
                for j in range(4):
                    first = i * TILE_B + j * BLK_B
                    sp.dma_start(x_cols[i][:, j, :], emb_rows[first:first + BLK_B]).then_inc(x_loaded[i], 16)

            def spread_tile(tile, i):
                copied, stored = value(sp, tile + 1), value(sp, tile * 16)
                used = value(sp, (tile - 1) * PAIRK)
                sp.wait_ge(x_rep_ready, copied)
                sp.dma_start(x_wide[bass.ds(tile, 1), :, :].rearrange("o r c -> (o r) c"), x_rep[i % 2][0:XT_ROWS, :]
                             ).then_inc(wide_stored, 16)
                wait(sp, pairs_ready, used)
                sp.wait_ge(wide_stored, stored)
                for r in range(REP):
                    steps = len(range(r, SHIFTS, REP))
                    first = x_wide[bass.ds(tile, 1), r:r + F, :].rearrange("o r c -> (o r) c")
                    src = bass.AP(first.tensor, first.offset, [[COLS, F], [REP * COLS, steps], [1, COLS]])
                    sp.dma_start(partners[i % 2][r * F:(r + 1) * F, 0:steps, :], src
                                 ).then_inc(partners_loaded[i % 2], 16)

            load_tile(0, 0)
            load_tile(0, 1)
            sp.wait_ge(w0_lo_ready, 1)
            spread_tile(1, 1)

            def quad(u, first, last):
                load_tile(u, 2)
                spread_tile(u * TILES + 2, 2)
                load_tile(u, 3)
                spread_tile(u * TILES + 3, 3)
                if not last:
                    load_tile(u + 1, 0)
                    load_tile(u + 1, 1)
                    spread_tile((u + 1) * TILES, 0)
                    spread_tile((u + 1) * TILES + 1, 1)

            over_quads(sp, quad)
            sp.wait_ge(y_copied, QUADS)
            sp.dma_start(out, y).then_inc(out_stored, 16)
            sp.wait_ge(out_stored, 16)

        @block.gpsimd
        def _(pool):
            def gather(u, f):
                pool.indirect_dma_start(
                    emb[:, f, :], None, tables[f],
                    bass.IndirectOffsetOnAxis(ap=next_ids[:, f:f + 1], axis=0)).then_inc(gathered, 16)

            def add_parts(u, n):
                g, v, out4 = u * BLOCKS + n, parts[n % 2], tails[n % 2]
                pool.wait_ge(prod_done, (g + 1) * len(A_PIECES))
                pool.wait_ge(acc_done, (g + 1) * D_OPS)
                pool.tensor_tensor(v[:, 0:8], v[:, 0:8], v[:, 8:16], ALU.add).then_inc(tree_done, 1)
                pool.wait_ge(tree_done, g * TREE + 1)
                pool.tensor_tensor(v[:, 0:4], v[:, 0:4], v[:, 4:8], ALU.add).then_inc(tree_done, 1)
                wait(pool, cur2_ready, g - 1)
                pool.wait_ge(tree_done, g * TREE + 2)
                pool.tensor_tensor(out4[:], v[:, 0:4], v[:, 16:20], ALU.add).then_inc(tree_done, 1)

            def make_x_diag(u, n):
                g = u * BLOCKS + n
                wait(pool, g_ready, g - 1)
                x = x_cols[n // 4][:, n % 4, ONE - F:ONE + 1]
                pool.tensor_tensor(x_diag[n % 2][:], x.unsqueeze(2).to_broadcast([P, FX, BLK_B]),
                                   blockmask[:].unsqueeze(1).to_broadcast([P, FX, BLK_B]), ALU.mult
                                   ).then_inc(x_diag_ready, 1)

            next_ids = sb("next_ids", [P, F], I32)
            ids_moved = sem("ids_moved")

            def move_ids(u):
                pool.tensor_copy(next_ids[:], ids[:, u, :]).then_inc(ids_moved, 1)
                pool.wait_ge(ids_moved, u + 1)

            pool.memset(emb_rows[:, :, ONE:ONE + 1], 1.0).then_inc(ones_set, 1)
            pool.wait_ge(ids_loaded, 16)
            move_ids(0)
            for f in range(F):
                gather(0, f)
            pool.wait_ge(gathered, F * 16)
            pool.wait_ge(rows_copied, 1)
            move_ids(1)
            for f in range(AHEAD):
                gather(1, f)

            def quad(u, first, last):
                for n in range(0 if first else -EARLY, BLOCKS - EARLY):
                    k = n + EARLY
                    if first:
                        shares = range(min(F, AHEAD + 2 * n), min(F, AHEAD + 2 * n + 2))
                    elif k > 0 and not last:
                        shares = range(min(F, F * (k - 1) // GATHER_BLOCKS), min(F, F * k // GATHER_BLOCKS))
                    else:
                        shares = ()
                    for f in shares:
                        gather(u + 1, f)
                    add_parts(u, n)
                    if k == 0 and not last:
                        pool.wait_ge(gathered, (u + 1) * F * 16)
                        pool.wait_ge(rows_copied, u + 1)
                        move_ids(u + 1)
                    make_x_diag(u, n)

            pool.wait_ge(const_loaded, 3 * 16)
            over_quads(pool, quad)
            for n in range(BLOCKS - EARLY, BLOCKS - 1):
                add_parts(QUADS - 1, n)
                make_x_diag(QUADS - 1, n)
            make_x_diag(QUADS - 1, BLOCKS - 1)

        @block.scalar
        def _(act):
            def copy_rows(u, r):
                if r == 0:
                    act.wait_ge(gathered, (u + 1) * F * 16)
                    for i in range(TILES):
                        wait(act, x_loaded[i], u * 4 * 16)
                last = nc.scalar.activation(emb_rows[:, :, r * F:(r + 1) * F], emb[:].rearrange("p f d -> p d f"),
                                            ACT.Copy)
                if r == REP - 1:
                    last.then_inc(rows_copied, 1)

            def weigh_piece(u, n, q):
                g, i = u * BLOCKS + n, A_PIECES.index(q)
                k = g * len(A_PIECES) + i
                if i == 0:
                    wait(act, tree_done, (g - 1) * TREE)
                    act.wait_ge(x_loaded[n // 4], (u + 1) * 4 * 16)
                act.wait_ge(l2a_ready, k + 1)
                src = pieces[(n * PIECES + q) % BANKS]
                for r in range(4):
                    f = 4 * q + r
                    last = nc.scalar.activation(parts[n % 2][:, 4 * i + r, :], src[:, r * H:(r + 1) * H], ACT.Copy,
                                                scale=x_cols[n // 4][:, n % 4, f:f + 1])
                last.then_inc(prod_done, 1)

            def copy_x_rep(tile, i):
                act.wait_ge(transposed, tile + 1)
                wait(act, pairs_ready, (tile - 1) * PAIRK)
                wait(act, wide_stored, (tile - 2) * 16)
                nc.scalar.activation(x_rep[i % 2][:], xbank[0:KPART, :], ACT.Copy).then_inc(x_rep_ready, 1)

            def take_pairs_high(tile, i, k):
                g, buf, rows = tile * PAIRK + k, (i * PAIRK + k) % 2, rows_of(k)
                act.wait_ge(pairs_ready, g + 1)
                wait(act, pairs_used, g - 1)
                nc.scalar.activation(pairs_hi[buf][0:rows, :], pairs[buf][0:rows, :], ACT.Copy
                                     ).then_inc(pairs_hi_ready, 1)

            def copy_cur1_hi(tile, i):
                act.wait_ge(pairs_used, (tile + 1) * PAIRK)
                wait(act, l2d_ready, (tile - 1) * 4 * len(D_PIECES))
                nc.scalar.activation(cur1_hi[i % 2][:], cur1_bank[:], ACT.Copy).then_inc(cur1_hi_ready, 1)

            def copy_g(u, n):
                g = u * BLOCKS + n
                act.wait_ge(g_ready, g + 1)
                if n == 0:
                    wait(act, l3_copied, u)
                dst = G[:, n // 4, :, (n % 4) * BLK_B:(n % 4 + 1) * BLK_B]
                nc.scalar.activation(dst, gbank[:, 0:FX * BLK_B].rearrange("p (f b) -> p f b", b=BLK_B),
                                     ACT.Copy).then_inc(g_copied, 1)

            def copy_l3(u):
                act.wait_ge(l3_ready, u + 1)
                wait(act, y_ready, u)
                nc.scalar.activation(sum2.rearrange("p (t b) -> p t b", b=TILE_B), G[:, :, F, :], ACT.Copy)
                nc.scalar.activation(sum3, xbank[:, 0:P], ACT.Copy).then_inc(l3_copied, 1)

            def relu1(u, half, sums=h_sums):
                act.wait_ge(h1_ready, u + 1)
                wait(act, h2_ready, u)
                for m in range(half * N1 // P // 2, (half + 1) * N1 // P // 2):
                    last = nc.scalar.activation(h1[:, m, :], sums[m], ACT.Relu,
                                                bias=bt1[:, m:m + 1])
                last.then_inc(h1_copied, 1)

            def relu2(u, sums=h_sums):
                act.wait_ge(h2_ready, u + 1)
                act.wait_ge(h1_ready, u + 1)
                for m in range(N2 // P):
                    last = nc.scalar.activation(h2[:, m, :], sums[m], ACT.Relu,
                                                bias=bt2[:, m:m + 1])
                last.then_inc(h2_copied, 1)

            def copy_y(u):
                act.wait_ge(y_ready, u + 1)
                nc.scalar.activation(sum1[0:1, bass.ds(u * P, P)], xbank[0:1, 0:P], ACT.Copy).then_inc(y_copied, 1)

            act.wait_ge(w1_loaded, 2 * 16)
            for part, cols in w1_raw:
                last = nc.scalar.activation(w1_hi[:, cols], part.rearrange("p f m -> p (f m)"), ACT.Copy)
            last.then_inc(w1_hi_ready, 1)
            act.wait_ge(w0_summed, 1)
            nc.scalar.activation(w0_hi[:, 0:PAIRK - 1, :], w0_raw[:, 0:PAIRK - 1, :], ACT.Copy)
            nc.scalar.activation(w0_hi[0:LAST_ROWS, PAIRK - 1, :], w0_raw[0:LAST_ROWS, PAIRK - 1, :], ACT.Copy
                                 ).then_inc(w0_hi_ready, 1)
            act.wait_ge(ones_set, 1)
            for r in range(REP):
                copy_rows(0, r)
            copy_x_rep(0, 0)
            copy_x_rep(1, 1)
            for k in range(PAIRK):
                take_pairs_high(0, 0, k)
            copy_cur1_hi(0, 0)
            act.wait_ge(w1_lo_ready, 1)
            act.wait_ge(top_loaded, 8 * 16)

            def quad(u, first, last):
                for i in range(TILES):
                    tile, more = u * TILES + i, not (last and i == TILES - 1)
                    for s in range(4 * PIECES):
                        n, q = 4 * i + s // PIECES, s % PIECES
                        if q in A_PIECES:
                            weigh_piece(u, n, q)
                        if more and s in S_HIGH:
                            take_pairs_high(tile + 1, i + 1, S_HIGH.index(s))
                        if s == S_T[i] + 1 and not (last and i >= TILES - 2):
                            copy_x_rep(tile + 2, i + 2)
                        if s - 1 in (S_G_FIRST if i == 0 else S_G):
                            if n >= G_LAG:
                                copy_g(u, n - G_LAG)
                            elif not first:
                                copy_g(u - 1, BLOCKS + n - G_LAG)
                        at = 4 * PIECES * i + s
                        if not first:
                            if at == S_L3_COPY:
                                copy_l3(u - 1)
                            if at in S_RELU1:
                                relu1(u - 1, S_RELU1.index(at))
                            if at == S_RELU2:
                                relu2(u - 1)
                            if at - 1 == S_Y:
                                copy_y(u - 1)
                        if i == 2 and s in S_ROWS and not last:
                            copy_rows(u + 1, S_ROWS.index(s))
                        if more and s == S_SUM[-1] + 1:
                            copy_cur1_hi(tile + 1, i + 1)

            over_quads(act, quad)
            u = QUADS - 1
            for n in range(BLOCKS - G_LAG, BLOCKS):
                copy_g(u, n)
            copy_l3(u)
            relu1(u, 0, h1_last)
            relu1(u, 1, h1_last)
            relu2(u, h2_last)
            copy_y(u)

        @block.vector
        def _(dve):
            def sum_piece(u, n, q):
                g, i = u * BLOCKS + n, D_PIECES.index(q)
                if i == 0:
                    dve.wait_ge(prod_done, g * len(A_PIECES) + 1)
                dve.wait_ge(l2d_ready, g * len(D_PIECES) + i + 1)
                src = pieces[(n * PIECES + q) % BANKS]
                for r in range(min(4, F - 4 * q)):
                    f, e = 4 * q + r, 4 * i + r
                    acc = parts[n % 2][:, r, :]
                    if i > 0 and r % 2 == 0:
                        dve.wait_ge(acc_done, g * D_OPS + min(e - 2, D_OPS))
                    nc.vector.scalar_tensor_tensor(acc, src[:, r * H:(r + 1) * H], x_cols[n // 4][:, n % 4, f:f + 1],
                                                   acc, ALU.mult, ALU.add).then_inc(acc_done, 1)

            def make_pairs(tile, i, k):
                g, buf, rows = tile * PAIRK + k, (i * PAIRK + k) % 2, rows_of(k)
                if k == 0:
                    dve.wait_ge(x_rep_ready, tile + 1)
                    dve.wait_ge(partners_loaded[i % 2], (tile - i % 2) * 8 * REP + i % 2 * 16 * REP)
                wait(dve, pairs_lo_ready, g - 1)
                nc.vector.tensor_tensor(pairs[buf][0:rows, :], partners[i % 2][0:rows, k, :], x_rep[i % 2][0:rows, :],
                                        ALU.mult).then_inc(pairs_ready, 1)

            def make_first_pairs(k):
                rows = rows_of(k)
                dve.wait_ge(x_rep_ready, 1)
                dve.wait_ge(first_partners, k + 1)
                wait(dve, pairs_lo_ready, k - 1)
                nc.vector.tensor_tensor(pairs[k % 2][0:rows, :], pieces[k % BANKS][0:rows, :], x_rep[0][0:rows, :],
                                        ALU.mult).then_inc(pairs_ready, 1)

            def take_pairs_low(tile, i, k):
                g, buf, rows = tile * PAIRK + k, (i * PAIRK + k) % 2, rows_of(k)
                dve.wait_ge(pairs_hi_ready, g + 1)
                wait(dve, pairs_used, g - 1)
                nc.vector.tensor_tensor(pairs_lo[buf][0:rows, :], pairs[buf][0:rows, :],
                                        pairs_hi[buf][0:rows, :].bitcast(FP32), ALU.subtract
                                        ).then_inc(pairs_lo_ready, 1)

            def take_cur1(tile, col, i):
                dve.wait_ge(cur1_hi_ready, tile + 1)
                nc.vector.tensor_tensor(cur1_lo[i % 2][:], cur1_bank[:], cur1_hi[i % 2][:].bitcast(FP32),
                                        ALU.subtract).then_inc(cur1_lo_ready, 1)
                nc.vector.tensor_reduce(sum1[:, bass.ds(col, TILE_B)],
                                        cur1_bank[:].rearrange("p (b d) -> p b d", d=D), AX.X, ALU.add
                                        ).then_inc(sum1_ready, 1)

            def add_last_parts():
                g, v, out4 = QUADS * BLOCKS - 1, parts[(BLOCKS - 1) % 2], tails[(BLOCKS - 1) % 2]
                dve.wait_ge(prod_done, (g + 1) * len(A_PIECES))
                dve.wait_ge(acc_done, (g + 1) * D_OPS)
                nc.vector.tensor_tensor(v[:, 0:8], v[:, 0:8], v[:, 8:16], ALU.add).then_inc(tree_done, 1)
                dve.wait_ge(tree_done, g * TREE + 1)
                nc.vector.tensor_tensor(v[:, 0:4], v[:, 0:4], v[:, 4:8], ALU.add).then_inc(tree_done, 1)
                dve.wait_ge(cur2_ready, g - 1)
                dve.wait_ge(tree_done, g * TREE + 2)
                nc.vector.tensor_tensor(out4[:], v[:, 0:4], v[:, 16:20], ALU.add).then_inc(tree_done, 1)

            def halve_tails(u, n):
                g, v = u * BLOCKS + n, tails[n % 2]
                dve.wait_ge(tree_done, (g + 1) * TREE)
                nc.vector.tensor_tensor(v[:, 0:2], v[:, 0:2], v[:, 2:4], ALU.add).then_inc(halved, 1)

            def finish_cur2(u, n):
                g, v = u * BLOCKS + n, tails[n % 2]
                wait(dve, g_ready, g - 1)
                dve.wait_ge(halved, g + 1)
                nc.vector.tensor_tensor(cur2[n % 2][:], v[:, 0], v[:, 1], ALU.add).then_inc(cur2_ready, 1)

            nc.vector.memset(w0_swapped[0:F, 0, :], 0.0).then_inc(zeros_set, 1)
            dve.wait_ge(w0_loaded, 5 * 16)
            dve.wait_ge(zeros_set, 1)
            for rows, ks in ((KPART, slice(0, PAIRK - 1)), (LAST_ROWS, slice(PAIRK - 1, PAIRK))):
                last = nc.vector.tensor_tensor(w0_raw[0:rows, ks, :], w0_raw[0:rows, ks, :], w0_swapped[0:rows, ks, :],
                                               ALU.add)
            last.then_inc(w0_summed, 1)
            dve.wait_ge(w0_hi_ready, 1)
            for rows, ks in ((KPART, slice(0, PAIRK - 1)), (LAST_ROWS, slice(PAIRK - 1, PAIRK))):
                last = nc.vector.tensor_tensor(w0_lo[0:rows, ks, :], w0_raw[0:rows, ks, :],
                                               w0_hi[0:rows, ks, :].bitcast(FP32), ALU.subtract)
            last.then_inc(w0_lo_ready, 1)
            dve.wait_ge(w1_hi_ready, 1)
            for part, cols in w1_raw:
                last = nc.vector.tensor_tensor(w1_lo[:, cols], part.rearrange("p f m -> p (f m)"),
                                               w1_hi[:, cols].bitcast(FP32), ALU.subtract)
            last.then_inc(w1_lo_ready, 1)
            make_first_pairs(0)
            for k in range(1, PAIRK):
                make_first_pairs(k)
                take_pairs_low(0, 0, k - 1)
            take_pairs_low(0, 0, PAIRK - 1)
            take_cur1(0, 0, 0)

            def quad(u, first, last):
                for i in range(TILES):
                    tile, more = u * TILES + i, not (last and i == TILES - 1)
                    for s in range(4 * PIECES):
                        n, q = 4 * i + s // PIECES, s % PIECES
                        if q in D_PIECES:
                            sum_piece(u, n, q)
                        if q in (Q_HALVE, Q_FINISH):
                            step = halve_tails if q == Q_HALVE else finish_cur2
                            if n >= 2:
                                step(u, n - 2)
                            elif not first:
                                step(u - 1, BLOCKS + n - 2)
                        if more and s in S_PAIR:
                            make_pairs(tile + 1, i + 1, S_PAIR.index(s))
                        if more and s in S_LOW:
                            take_pairs_low(tile + 1, i + 1, S_LOW.index(s))
                        if more and s == S_SUM[-1] + 2:
                            take_cur1(tile + 1, (tile + 1) * TILE_B, i + 1)

            over_quads(dve, quad)
            halve_tails(QUADS - 1, BLOCKS - 2)
            finish_cur2(QUADS - 1, BLOCKS - 2)
            add_last_parts()
            halve_tails(QUADS - 1, BLOCKS - 1)
            finish_cur2(QUADS - 1, BLOCKS - 1)

        @block.tensor
        def _(pe):
            def transpose_x(tile, u, i, first=True):
                pe.wait_ge(x_loaded[i], (u + 1) * 4 * 16)
                wait(pe, x_rep_ready, tile)
                if i == 3 and not first:
                    pe.wait_ge(y_copied, u)
                for j in range(4):
                    last = nc.tensor.transpose(xbank[0:KPART, j * P:(j + 1) * P], x_cols[i][:, j, 0:KPART], ident[:])
                last.then_inc(transposed, 1)

            def shift_first(k):
                if k == 0:
                    pe.wait_ge(x_rep_ready, 1)
                wait(pe, pairs_ready, k - BANKS + 1)
                nc.tensor.matmul(pieces[k % BANKS][0:rows_of(k), :], shift_rows[:, k, 0:rows_of(k)], x_rep[0][0:F, :],
                                 start=True, stop=True).then_inc(first_partners, 1)

            def sum_pairs(tile, i, k):
                g, buf, rows = tile * PAIRK + k, (i * PAIRK + k) % 2, rows_of(k)
                pe.wait_ge(pairs_lo_ready, g + 1)
                if k == 0:
                    wait(pe, cur1_lo_ready, tile)
                    wait(pe, sum1_ready, tile)
                hi, lo = pairs_hi[buf][0:rows, :], pairs_lo[buf][0:rows, :]
                nc.tensor.matmul(cur1_bank[:], w0_hi[0:rows, k, :], hi, start=k == 0, stop=False)
                nc.tensor.matmul(cur1_bank[:], w0_lo[0:rows, k, :], hi, start=False, stop=False)
                nc.tensor.matmul(cur1_bank[:], w0_hi[0:rows, k, :], lo, start=False, stop=k == PAIRK - 1
                                 ).then_inc(pairs_used, 1)

            def layer2_piece(u, n, q):
                width = min(4, F - 4 * q) * H
                dst = pieces[(n * PIECES + q) % BANKS]
                g, back = (u * BLOCKS + n, q - BANKS) if q >= BANKS else (u * BLOCKS + n - 1, q - BANKS + PIECES)
                if back in D_PIECES:
                    wait(pe, acc_done, g * D_OPS + min(4 * (D_PIECES.index(back) + 1), D_OPS))
                else:
                    wait(pe, prod_done, g * len(A_PIECES) + A_PIECES.index(back) + 1)
                lo, hi = cur1_lo[n // 4 % 2], cur1_hi[n // 4 % 2]
                cols = slice(n % 4 * P, (n % 4 + 1) * P)
                ws = slice(4 * q * H, 4 * q * H + width)
                nc.tensor.matmul(dst[:, 0:width], hi[:, cols], w1_hi[:, ws], start=True, stop=False)
                nc.tensor.matmul(dst[:, 0:width], hi[:, cols], w1_lo[:, ws], start=False, stop=False)
                nc.tensor.matmul(dst[:, 0:width], lo[:, cols], w1_hi[:, ws], start=False, stop=True
                                 ).then_inc(l2d_ready if q in D_PIECES else l2a_ready, 1)

            def make_g(u, n):
                g = u * BLOCKS + n
                pe.wait_ge(cur2_ready, g + 1)
                pe.wait_ge(x_diag_ready, g + 1)
                wait(pe, g_copied, g)
                nc.tensor.matmul(gbank[:, 0:FX * BLK_B], cur2[n % 2][:], x_diag[n % 2][:].rearrange("p f b -> p (f b)"),
                                 start=True, stop=True).then_inc(g_ready, 1)

            def layer3(u, step, tiles):
                if step == 0:
                    pe.wait_ge(g_copied, (u + 1) * BLOCKS)
                    pe.wait_ge(x_rep_ready, tiles)
                for f in range(step * L3_STEP, (step + 1) * L3_STEP):
                    last = nc.tensor.matmul(xbank[:, 0:P], w2[:, f, :], G[:, :, f, :], start=f == 0, stop=f == F - 1)
                if step == F // L3_STEP - 1:
                    last.then_inc(l3_ready, 1)

            def top1_early(u, m, sums):
                dst, ms = sums[m], slice(m * P, (m + 1) * P)
                if m == 0:
                    pe.wait_ge(sum1_ready, (u + 1) * TILES)
                nc.tensor.matmul(dst, wt1[:, 0, ms], sum1[:, bass.ds(u * P, P)], start=True, stop=False)
                nc.tensor.matmul(dst, wt1_dense[:, ms], dense[:, bass.ds(u * P, P)], start=False, stop=False)

            def top1_late(u, m, sums):
                dst, ms = sums[m], slice(m * P, (m + 1) * P)
                nc.tensor.matmul(dst, wt1[:, 1, ms], sum2, start=False, stop=False)
                last = nc.tensor.matmul(dst, wt1[:, 2, ms], sum3, start=False, stop=True)
                if m == N1 // P - 1:
                    last.then_inc(h1_ready, 1)

            def top2(u, m, sums=h_sums):
                pe.wait_ge(h1_copied, (u + 1) * 2)
                for k in range(N1 // P):
                    last = nc.tensor.matmul(sums[m], wt2[:, k, m * P:(m + 1) * P], h1[:, k, :],
                                            start=k == 0, stop=k == N1 // P - 1)
                if m == N2 // P - 1:
                    last.then_inc(h2_ready, 1)

            def top3(u):
                pe.wait_ge(h2_copied, u + 1)
                for k in range(N2 // P):
                    last = nc.tensor.matmul(xbank[0:1, 0:P], wt3[:, k:k + 1], h2[:, k, :], start=k == 0,
                                            stop=k == N2 // P - 1)
                last.then_inc(y_ready, 1)

            def warm_up(count, bank):
                for _ in range(count):
                    nc.tensor.matmul(bank[:], w1_hi[:, 0:P], w1_hi[:, 0:512], start=True, stop=True)

            pe.wait_ge(w1_hi_ready, 1)
            pe.wait_ge(gathered, F * 16)
            warm_up(WARM_UP, pieces[0])
            pe.wait_ge(const_loaded, 3 * 16)
            transpose_x(0, 0, 0)
            warm_up(4, pieces[0])
            pe.wait_ge(w0_hi_ready, 1)
            pe.wait_ge(w0_lo_ready, 1)
            ahead = BANKS
            for k in range(ahead):
                shift_first(k)
                if k == 1:
                    transpose_x(1, 0, 1)
            for k in range(PAIRK):
                sum_pairs(0, 0, k)
                if k + ahead < PAIRK:
                    shift_first(k + ahead)
            warm_up(6, pieces[4])
            pe.wait_ge(w1_hi_ready, 1)
            pe.wait_ge(w1_lo_ready, 1)
            pe.wait_ge(top_loaded, 8 * 16)

            def quad(u, first, last):
                for i in range(TILES):
                    tile, more = u * TILES + i, not (last and i == TILES - 1)
                    nu, ni = (u, i + 2) if i < TILES - 2 else (u + 1, i + 2 - TILES)
                    pe.wait_ge(cur1_hi_ready, tile + 1)
                    pe.wait_ge(cur1_lo_ready, tile + 1)
                    for s in range(4 * PIECES):
                        n, q = 4 * i + s // PIECES, s % PIECES
                        layer2_piece(u, n, q)
                        if s == S_T[i] and not (last and i >= TILES - 2):
                            transpose_x(tile + 2, nu, ni, first)
                        if more and s in S_SUM:
                            sum_pairs(tile + 1, i + 1, S_SUM.index(s))
                        if s in (S_G_FIRST if i == 0 else S_G):
                            if n >= G_LAG:
                                make_g(u, n - G_LAG)
                            elif not first:
                                make_g(u - 1, BLOCKS + n - G_LAG)
                        at = 4 * PIECES * i + s
                        if not first:
                            if at in S_L3:
                                layer3(u - 1, S_L3.index(at), u * TILES + 3)
                            if at in S_H1:
                                if at == S_H1[0]:
                                    pe.wait_ge(l3_copied, u)
                                top1_early(u - 1, S_H1.index(at), h_sums)
                                top1_late(u - 1, S_H1.index(at), h_sums)
                            if at in S_H2:
                                top2(u - 1, S_H2.index(at))
                            if at == S_Y:
                                top3(u - 1)

            over_quads(pe, quad)
            u = QUADS - 1
            pe.wait_ge(cur1_lo_ready, QUADS * TILES)
            pe.wait_ge(sum1_ready, QUADS * TILES)
            warm_up(4, cur1_bank)
            make_g(u, BLOCKS - 3)
            warm_up(4, cur1_bank)
            make_g(u, BLOCKS - 2)
            pe.wait_ge(acc_done, QUADS * BLOCKS * D_OPS)
            pe.wait_ge(prod_done, QUADS * BLOCKS * len(A_PIECES))
            for m in range(N1 // P):
                top1_early(u, m, h1_last)
            warm_up(5, cur1_bank)
            make_g(u, BLOCKS - 1)
            for step in range(F // L3_STEP):
                layer3(u, step, QUADS * TILES)
            pe.wait_ge(l3_copied, u + 1)
            for m in range(N1 // P):
                top1_late(u, m, h1_last)
            for m in range(N2 // P):
                top2(u, m, h2_last)
            top3(u)


def kernel(**inputs):
    import numpy as np
    import concourse.bacc as bacc
    from concourse.bass_utils import run_bass_kernel_spmd

    i = np.arange(F)
    w0 = np.asarray(inputs["L0_rec_f0"])
    rows = np.concatenate([i * F + (i + s) % F for s in range(SHIFTS)])
    swapped = np.concatenate([(i + s) % F * F + i for s in range(1, SHIFTS)])

    blockmask = np.repeat(np.eye(BLK_B, dtype=np.float32), D, axis=0)

    k, row = np.arange(PAIRK)[:, None], np.arange(KPART)[None, :]
    source = (row % F + REP * k + row // F) % F
    shift_rows = (np.arange(F)[:, None, None] == source).astype(np.float32)

    def by_partition(v):
        return np.ascontiguousarray(np.asarray(v).reshape(-1, P).T)

    arrays = {
        "ids": np.asarray(inputs["ids"]),
        "w0": w0[rows], "w0_swapped": w0[swapped],
        "w1": np.asarray(inputs["L0_rec_f1"]), "w2": np.asarray(inputs["L0_rec_f2"]),
        "wt1": np.asarray(inputs["W_top1"]), "bt1": by_partition(inputs["b_top1"]),
        "wt2": np.asarray(inputs["W_top2"]), "bt2": by_partition(inputs["b_top2"]),
        "wt3": by_partition(inputs["W_top3"]),
        "dense": np.ascontiguousarray(np.asarray(inputs["dense_ctx"]).T),
        "ident": np.eye(P, dtype=np.float32), "blockmask": blockmask,
        "shift_rows": shift_rows,
    }
    for f in range(F):
        arrays[f"tbl_{f}"] = np.asarray(inputs[f"tbl_{f}"])

    nc = bacc.Bacc("TRN2", target_bir_lowering=False, num_devices=1)
    t = {k: nc.dram_tensor(f"in_{k}", v.shape, mybir.dt.from_np(v.dtype), kind="ExternalInput").ap()
         for k, v in arrays.items()}
    t["x_wide"] = nc.dram_tensor("x_wide", (B // TILE_B, XT_ROWS, COLS), FP32, kind="Internal").ap()
    out = nc.dram_tensor("out", (1, B), FP32, kind="ExternalOutput").ap()
    cin_kernel(nc, t, [t[f"tbl_{f}"] for f in range(F)], out)
    r = run_bass_kernel_spmd(nc, [{f"in_{k}": v for k, v in arrays.items()}], core_ids=[0])
    return r.results[0]["out"].reshape(B, 1)
```
